# Optimizing a Trainium2 kernel written in Bass

```python
import numpy as np
import jax
import jax.numpy as jnp

def _softmax(x, axis=-1):
    return jax.nn.softmax(x, axis=axis)

def _gelu(x):
    return jax.nn.gelu(x, approximate=True)

def _silu(x):
    return jax.nn.silu(x)

def _sigmoid(x):
    return jax.nn.sigmoid(x)

def _layernorm(x, axis=-1, eps=1e-05):
    m = jnp.mean(x, axis=axis, keepdims=True)
    v = jnp.var(x, axis=axis, keepdims=True)
    return (x - m) / jnp.sqrt(v + eps)

def _scatter_add(tgt, idx, src, axis=0):
    return tgt.at[idx].add(src)

def _segment_sum(src, seg, n):
    return jax.ops.segment_sum(src, seg, n)
kernel_name = 'mk_dlrm_tower_d1_rec_r8_f699b3'

def setup_inputs(seed: int=0):
    np.random.seed(seed)
    _w = jnp.asarray

    def _rec_inputs():
        import jax
        import jax.numpy as jnp
        _tk = jax.random.key(seed)
        dense_ctx = jax.random.normal(jax.random.fold_in(_tk, 190), (2048, 16), jnp.float32)
        ids = jnp.stack([jax.random.randint(jax.random.fold_in(_tk, 200 + f), (2048,), 0, v, jnp.int32) for f, v in enumerate([125000, 12500, 12500, 1000, 12500, 1000, 12500, 1000, 1000, 12500, 1250, 1000, 12500, 1000, 1000, 1000, 1250, 12500, 1250, 12500, 12500, 1250, 1000, 1000, 1000, 1000, 1000])], axis=1)
        tbl_0 = 0.05 * jax.random.normal(jax.random.fold_in(_tk, 500 + 0), (125000, 128), jnp.float32)
        tbl_1 = 0.05 * jax.random.normal(jax.random.fold_in(_tk, 500 + 1), (12500, 128), jnp.float32)
        tbl_2 = 0.05 * jax.random.normal(jax.random.fold_in(_tk, 500 + 2), (12500, 128), jnp.float32)
        tbl_3 = 0.05 * jax.random.normal(jax.random.fold_in(_tk, 500 + 3), (1000, 128), jnp.float32)
        tbl_4 = 0.05 * jax.random.normal(jax.random.fold_in(_tk, 500 + 4), (12500, 128), jnp.float32)
        tbl_5 = 0.05 * jax.random.normal(jax.random.fold_in(_tk, 500 + 5), (1000, 128), jnp.float32)
        tbl_6 = 0.05 * jax.random.normal(jax.random.fold_in(_tk, 500 + 6), (12500, 128), jnp.float32)
        tbl_7 = 0.05 * jax.random.normal(jax.random.fold_in(_tk, 500 + 7), (1000, 128), jnp.float32)
        tbl_8 = 0.05 * jax.random.normal(jax.random.fold_in(_tk, 500 + 8), (1000, 128), jnp.float32)
        tbl_9 = 0.05 * jax.random.normal(jax.random.fold_in(_tk, 500 + 9), (12500, 128), jnp.float32)
        tbl_10 = 0.05 * jax.random.normal(jax.random.fold_in(_tk, 500 + 10), (1250, 128), jnp.float32)
        tbl_11 = 0.05 * jax.random.normal(jax.random.fold_in(_tk, 500 + 11), (1000, 128), jnp.float32)
        tbl_12 = 0.05 * jax.random.normal(jax.random.fold_in(_tk, 500 + 12), (12500, 128), jnp.float32)
        tbl_13 = 0.05 * jax.random.normal(jax.random.fold_in(_tk, 500 + 13), (1000, 128), jnp.float32)
        tbl_14 = 0.05 * jax.random.normal(jax.random.fold_in(_tk, 500 + 14), (1000, 128), jnp.float32)
        tbl_15 = 0.05 * jax.random.normal(jax.random.fold_in(_tk, 500 + 15), (1000, 128), jnp.float32)
        tbl_16 = 0.05 * jax.random.normal(jax.random.fold_in(_tk, 500 + 16), (1250, 128), jnp.float32)
        tbl_17 = 0.05 * jax.random.normal(jax.random.fold_in(_tk, 500 + 17), (12500, 128), jnp.float32)
        tbl_18 = 0.05 * jax.random.normal(jax.random.fold_in(_tk, 500 + 18), (1250, 128), jnp.float32)
        tbl_19 = 0.05 * jax.random.normal(jax.random.fold_in(_tk, 500 + 19), (12500, 128), jnp.float32)
        tbl_20 = 0.05 * jax.random.normal(jax.random.fold_in(_tk, 500 + 20), (12500, 128), jnp.float32)
        tbl_21 = 0.05 * jax.random.normal(jax.random.fold_in(_tk, 500 + 21), (1250, 128), jnp.float32)
        tbl_22 = 0.05 * jax.random.normal(jax.random.fold_in(_tk, 500 + 22), (1000, 128), jnp.float32)
        tbl_23 = 0.05 * jax.random.normal(jax.random.fold_in(_tk, 500 + 23), (1000, 128), jnp.float32)
        tbl_24 = 0.05 * jax.random.normal(jax.random.fold_in(_tk, 500 + 24), (1000, 128), jnp.float32)
        tbl_25 = 0.05 * jax.random.normal(jax.random.fold_in(_tk, 500 + 25), (1000, 128), jnp.float32)
        tbl_26 = 0.05 * jax.random.normal(jax.random.fold_in(_tk, 500 + 26), (1000, 128), jnp.float32)
        _rk = jax.random.fold_in(_tk, 7)
        W_top1 = 0.0521996 * jax.random.normal(jax.random.fold_in(_tk, 801), (367, 512), jnp.float32)
        W_top2 = 0.0441942 * jax.random.normal(jax.random.fold_in(_tk, 802), (512, 256), jnp.float32)
        W_top3 = 0.0625 * jax.random.normal(jax.random.fold_in(_tk, 803), (256, 1), jnp.float32)
        b_top1 = jnp.zeros((512,), jnp.float32)
        b_top2 = jnp.zeros((256,), jnp.float32)
        return (dense_ctx, ids, tbl_0, tbl_1, tbl_2, tbl_3, tbl_4, tbl_5, tbl_6, tbl_7, tbl_8, tbl_9, tbl_10, tbl_11, tbl_12, tbl_13, tbl_14, tbl_15, tbl_16, tbl_17, tbl_18, tbl_19, tbl_20, tbl_21, tbl_22, tbl_23, tbl_24, tbl_25, tbl_26, W_top1, b_top1, W_top2, b_top2, W_top3)
    dense_ctx, ids, tbl_0, tbl_1, tbl_2, tbl_3, tbl_4, tbl_5, tbl_6, tbl_7, tbl_8, tbl_9, tbl_10, tbl_11, tbl_12, tbl_13, tbl_14, tbl_15, tbl_16, tbl_17, tbl_18, tbl_19, tbl_20, tbl_21, tbl_22, tbl_23, tbl_24, tbl_25, tbl_26, W_top1, b_top1, W_top2, b_top2, W_top3 = _rec_inputs()

    def _L0_rec_setup():
        import jax, jax.numpy as jnp
        import numpy as np
        NUM_FEATURES = 27
        EMBED_DIM = 128
        BATCH = 4096
        key = jax.random.key(seed)
        inputs = jax.random.normal(key, (BATCH, NUM_FEATURES, EMBED_DIM), dtype=jnp.float32)
        return {'inputs': inputs}
    _L0_rec_all = _L0_rec_setup()
    _L0_rec_in = {k: v for k, v in _L0_rec_all.items() if k in ()}
    del _L0_rec_all
    return {'dense_ctx': dense_ctx, 'ids': ids, 'tbl_0': tbl_0, 'tbl_1': tbl_1, 'tbl_2': tbl_2, 'tbl_3': tbl_3, 'tbl_4': tbl_4, 'tbl_5': tbl_5, 'tbl_6': tbl_6, 'tbl_7': tbl_7, 'tbl_8': tbl_8, 'tbl_9': tbl_9, 'tbl_10': tbl_10, 'tbl_11': tbl_11, 'tbl_12': tbl_12, 'tbl_13': tbl_13, 'tbl_14': tbl_14, 'tbl_15': tbl_15, 'tbl_16': tbl_16, 'tbl_17': tbl_17, 'tbl_18': tbl_18, 'tbl_19': tbl_19, 'tbl_20': tbl_20, 'tbl_21': tbl_21, 'tbl_22': tbl_22, 'tbl_23': tbl_23, 'tbl_24': tbl_24, 'tbl_25': tbl_25, 'tbl_26': tbl_26, 'W_top1': W_top1, 'b_top1': b_top1, 'W_top2': W_top2, 'b_top2': b_top2, 'W_top3': W_top3}

def reference(dense_ctx, ids, tbl_0, tbl_1, tbl_2, tbl_3, tbl_4, tbl_5, tbl_6, tbl_7, tbl_8, tbl_9, tbl_10, tbl_11, tbl_12, tbl_13, tbl_14, tbl_15, tbl_16, tbl_17, tbl_18, tbl_19, tbl_20, tbl_21, tbl_22, tbl_23, tbl_24, tbl_25, tbl_26, W_top1, b_top1, W_top2, b_top2, W_top3):
    import jax
    import jax.numpy as jnp

    def _L0_rec_ref(inputs):
        import jax, jax.numpy as jnp
        import numpy as np
        NUM_FEATURES = 27
        EMBED_DIM = 128
        BATCH = 4096
        interactions = jnp.einsum('bnd,bmd->bnm', inputs, inputs)
        n = inputs.shape[1]
        i, j = jnp.triu_indices(n, k=1)
        return interactions[:, i, j]
    e = jnp.stack([tbl_0[ids[:, 0]], tbl_1[ids[:, 1]], tbl_2[ids[:, 2]], tbl_3[ids[:, 3]], tbl_4[ids[:, 4]], tbl_5[ids[:, 5]], tbl_6[ids[:, 6]], tbl_7[ids[:, 7]], tbl_8[ids[:, 8]], tbl_9[ids[:, 9]], tbl_10[ids[:, 10]], tbl_11[ids[:, 11]], tbl_12[ids[:, 12]], tbl_13[ids[:, 13]], tbl_14[ids[:, 14]], tbl_15[ids[:, 15]], tbl_16[ids[:, 16]], tbl_17[ids[:, 17]], tbl_18[ids[:, 18]], tbl_19[ids[:, 19]], tbl_20[ids[:, 20]], tbl_21[ids[:, 21]], tbl_22[ids[:, 22]], tbl_23[ids[:, 23]], tbl_24[ids[:, 24]], tbl_25[ids[:, 25]], tbl_26[ids[:, 26]]], axis=1)
    z = _L0_rec_ref(e)
    z = z.reshape(z.shape[0], -1)
    h = jnp.concatenate([z, dense_ctx], axis=1)
    h = jnp.maximum(h @ W_top1 + b_top1, 0.0)
    h = jnp.maximum(h @ W_top2 + b_top2, 0.0)
    y = h @ W_top3
    return y

_drawn_inputs = setup_inputs


def setup_inputs(seed=0):
    import zlib

    import numpy as np

    out = dict(_drawn_inputs(seed))
    spreads = {'b_top1': (0.0, 0.1), 'b_top2': (0.0, 0.1)}
    factors = {}
    for name, (base, spread) in spreads.items():
        noise = np.random.default_rng([zlib.crc32(name.encode()), seed]).standard_normal(out[name].shape)
        drawn = base * np.exp(spread * noise) if base else spread * noise
        out[name] = jnp.asarray(drawn.astype(out[name].dtype))
    for name, factor in factors.items():
        out[name] = (out[name] * factor).astype(out[name].dtype)
    return out
```

```python
from contextlib import ExitStack

import numpy as np

import concourse.bass as bass
from concourse import mybir

F32 = mybir.dt.float32
F32R = mybir.dt.float32r
I32 = mybir.dt.int32
ALU = mybir.AluOpType
ACT = mybir.ActivationFunctionType

P = 128
QUAD = 32
NQ = P // QUAD
BATCH = 2048
NF = 27
DIM = 128
DENSE = 16
HID1, HID2 = 512, 256
TILES = 2
PAIR = TILES * P
PAIRS = BATCH // PAIR

VOCAB_ONEHOT = 1000
ROWS = 125
ROWS_PER = VOCAB_ONEHOT // ROWS
ONEHOT = [3, 5, 7, 8]
GATHERED = [f for f in range(NF) if f not in ONEHOT]
NG, NO = len(GATHERED), len(ONEHOT)
SLOT_FEATURE = GATHERED + ONEHOT

GROUP = NF // 3
BETWEEN, WITHIN = GROUP, GROUP - 1
STEPS = -(-(BETWEEN + WITHIN + 1) // NQ)
DENSE_COLUMN = BETWEEN + WITHIN

GRAMS = PAIR // NQ
PER_BANK = 4
GRAM_BATCHES = GRAMS // PER_BANK
GRAM_BANKS = 4
GCOLS = NQ * NF
TR_PER_BANK = 4
TR_SIZES = [min(TR_PER_BANK, NG - s) for s in range(0, NG, TR_PER_BANK)]
OH_SIZES = [min(2, NO - s) for s in range(0, NO, 2)]
EMB_BATCHES = TILES * len(TR_SIZES) + len(OH_SIZES)
EMB_BANKS = 2
M1, M2 = HID1 // P, HID2 // P
MLP_CHUNKS = M1 + M2 + 1
ONEHOT_RING = 2
GATHER_RING = 2 * TILES
FOLD_DVE, FOLD_ACT = (0, 1), (2, 3)
assert EMB_BATCHES % EMB_BANKS == 0


def fold_copies():
    rounds = []
    for rows, between, within in ((3, 0, 2), (2, 2, 1), (1, 1, 0)):
        copies = []
        for first, count, group in ((0, BETWEEN, between), (BETWEEN, WITHIN, within)):
            for k in range(NQ):
                n = len(range(k, count, NQ))
                quad, step = (first + k) % NQ, (first + k) // NQ
                copies.append((quad, step, n, rows * GROUP, group * GROUP + k))
        rounds.append(copies)
    return rounds


def folded_pairs():
    seen, out = set(), []
    for c in range(BETWEEN + WITHIN):
        for row in range(NF):
            g = row // GROUP
            other = ((g + 1) % 3) * GROUP + c if c < BETWEEN else g * GROUP + c - BETWEEN
            pair = frozenset((row, other))
            if row != other and pair not in seen:
                seen.add(pair)
                out.append((c, row, other))
    assert len(out) == NF * (NF - 1) // 2
    return out


def build(nc, dense_t, ids_rows, ids_onehot, gathered_tables, onehot_tables, w1, w2, w3, b1, b2, out):
    with ExitStack() as ctx:
        def sb(name, shape, dt=F32):
            return ctx.enter_context(nc.sbuf_tensor(name, shape, dt))

        def sem(name):
            return ctx.enter_context(nc.semaphore(name))

        idx = sb("idx", [P, 2, TILES * NG], I32)
        ids_b = sb("ids_b", [P, 2, NO, PAIR], I32)
        rows = sb("rows", [P, GATHER_RING, NG, DIM])
        emb = sb("emb", [P, TILES, P, QUAD])
        gram = sb("gram", [P, GRAM_BATCHES, PER_BANK * GCOLS])
        folded = sb("folded", [P, 2, STEPS, PAIR])
        table_hi = sb("table_hi", [P, NO, ROWS_PER, DIM], F32R)
        table_lo = sb("table_lo", [P, NO, ROWS_PER, DIM], F32R)
        onehot = sb("onehot", [P, ONEHOT_RING, ROWS_PER, PAIR], F32R)
        row_id_i = sb("row_id_i", [P, ROWS_PER], I32)
        row_id = sb("row_id", [P, ROWS_PER])
        ident = sb("ident", [P, P])
        w1_sb = sb("w1_sb", [P, STEPS, HID1])
        w2_sb = sb("w2_sb", [P, M1, HID2])
        w3_sb = sb("w3_sb", [P, M2])
        b1_sb = sb("b1_sb", [P, M1])
        b2_sb = sb("b2_sb", [P, M2])
        h1 = sb("h1", [P, M1, PAIR])
        h2 = sb("h2", [P, M2, PAIR])
        y = sb("y", [1, 2, PAIR])
        stage = emb[:, :, :, :].rearrange("p t b s -> p (t b s)")

        gram_ps = [ctx.enter_context(nc.psum_tensor(f"gram_ps{i}", [P, 512], F32)) for i in range(GRAM_BANKS)]
        emb_ps = [ctx.enter_context(nc.psum_tensor(f"emb_ps{i}", [P, 512], F32)) for i in range(EMB_BANKS)]
        mlp_ps = [ctx.enter_context(nc.psum_tensor(f"mlp_ps{i}", [P, 512], F32)) for i in range(2)]

        idx_loaded = [sem(f"idx_loaded{i}") for i in range(2)]
        ids_b_loaded = [sem(f"ids_b_loaded{i}") for i in range(2)]
        dense_loaded = [sem(f"dense_loaded{i}") for i in range(2)]
        table_loaded = [sem(f"table_loaded{i}") for i in range(NO)]
        weights_loaded = sem("weights_loaded")
        gathered = [sem(f"gathered{i}") for i in range(GATHER_RING)]
        gather_begun = sem("gather_begun")
        ident_steps = sem("ident_steps")
        split_steps = sem("split_steps")
        cleared = sem("cleared")
        onehot_ready = sem("onehot_ready")
        emb_ps_full = sem("emb_ps_full")
        emb_ps_empty = sem("emb_ps_empty")
        gram_ps_full = sem("gram_ps_full")
        gram_ps_empty = sem("gram_ps_empty")
        folded_dve = sem("folded_dve")
        folded_act = sem("folded_act")
        mlp_full = sem("mlp_full")
        mlp_empty = sem("mlp_empty")
        y_stored = [sem(f"y_stored{i}") for i in range(2)]

        ROUNDS = fold_copies()
        NR = len(ROUNDS)

        def pair(i, c):
            return i * 2 + c, c % 2, i + c // 2

        def fold_aps(par, q, copy):
            quad, step, n, nrows, src = copy
            dst = folded[quad * QUAD:quad * QUAD + nrows, par, step:step + n, :].rearrange(
                "p n (t g q) -> p n t g q", t=TILES, q=NQ)[:, :, :, :, q]
            col = q * NF + src
            products = gram[q * QUAD:q * QUAD + nrows, :, :].rearrange("p a (b c) -> p c (a b)", c=GCOLS)
            from_ = products[:, col:col + NQ * (n - 1) + 1:NQ, :].rearrange("p n (t g) -> p n t g", t=TILES)
            return dst, from_

        block = ctx.enter_context(nc.Block())

        @block.sync
        def _(sp):
            def load_idx(p, par):
                for t in range(TILES):
                    sp.dma_start(idx[:, par, t * NG:(t + 1) * NG],
                                 ids_rows[bass.ds(p * TILES + t, 1), :, :].rearrange("o p f -> (o p) f")
                                 ).then_inc(idx_loaded[par], 16)

            def load_ids_b(p, par):
                sp.dma_start(ids_b[:, par, :, :],
                             ids_onehot[:, bass.ds(p * PAIR, PAIR)].partition_broadcast(P)
                             ).then_inc(ids_b_loaded[par], 16)

            def load_dense(p, par):
                q, step = DENSE_COLUMN % NQ, DENSE_COLUMN // NQ
                sp.dma_start(folded[q * QUAD:q * QUAD + DENSE, par, step, :],
                             dense_t[:, bass.ds(p * PAIR, PAIR)]).then_inc(dense_loaded[par], 16)

            def load_ahead(p, par, use):
                for t in range(TILES):
                    sp.wait_ge(gathered[par * TILES + t], (use + 1) * (16 * NG))
                load_idx(p + 2, par)
                sp.wait_ge(onehot_ready, (p + 1) * NO)
                load_ids_b(p + 2, par)
                sp.wait_ge(mlp_full, p * MLP_CHUNKS + M1)
                load_dense(p + 2, par)

            def store_y(p, par):
                sp.wait_ge(mlp_empty, (p + 1) * MLP_CHUNKS)
                sp.dma_start(out[bass.ds(p * PAIR, PAIR), :].rearrange("n o -> o n"),
                             y[:, par, :]).then_inc(y_stored[par], 16)

            load_idx(0, 0)
            for n in range(NO):
                sp.dma_start(stage[0:ROWS, n * ROWS_PER * DIM:(n + 1) * ROWS_PER * DIM],
                             onehot_tables[n].rearrange("(p j) d -> p (j d)", j=ROWS_PER)
                             ).then_inc(table_loaded[n], 16)
            load_ids_b(0, 0)
            load_idx(1, 1)
            load_ids_b(1, 1)
            for dst, src in ((w1_sb, w1), (w2_sb, w2), (w3_sb, w3), (b1_sb, b1), (b2_sb, b2)):
                sp.dma_start(dst[:], src).then_inc(weights_loaded, 16)
            sp.wait_ge(cleared, 1)
            load_dense(0, 0)
            load_dense(1, 1)
            with sp.Fori(0, PAIRS // 2 - 1) as i:
                for c in range(2):
                    p, par, use = pair(i, c)
                    load_ahead(p, par, use)
                    store_y(p, par)
            for c in range(2):
                p, par, use = pair(PAIRS // 2 - 1, c)
                store_y(p, par)
            for par in range(2):
                sp.wait_ge(y_stored[par], 16 * (PAIRS // 2))

        @block.gpsimd
        def _(pool):
            def gather(p, par, use, reuse):
                for t in range(TILES):
                    pool.wait_ge(idx_loaded[par], (use + 1) * (16 * TILES))
                    if reuse:
                        pool.wait_ge(emb_ps_full,
                                     (p - 2) * EMB_BATCHES + len(OH_SIZES) + (t + 1) * len(TR_SIZES))
                    pool.sem_inc(gather_begun, 1)
                    slot = par * TILES + t
                    for n in range(NG):
                        col = t * NG + n
                        pool.indirect_dma_start(
                            out=rows[:, slot, n, :], out_offset=None, in_=gathered_tables[n],
                            in_offset=bass.IndirectOffsetOnAxis(ap=idx[:, par, col:col + 1], axis=0),
                        ).then_inc(gathered[slot], 16)

            nc.gpsimd.memset(ident[:], 0.0).then_inc(ident_steps, 1)
            nc.gpsimd.iota(row_id_i[:], pattern=[[1, ROWS_PER]], base=0,
                           channel_multiplier=ROWS_PER).then_inc(ident_steps, 1)
            pool.wait_ge(ident_steps, 2)
            nc.gpsimd.affine_select(out=ident[:], in_=ident[:], compare_op=ALU.not_equal, fill=1.0,
                                    base=0, pattern=[[-1, P]], channel_multiplier=1).then_inc(ident_steps, 1)
            for c in range(2):
                gather(*pair(0, c), reuse=False)
            with pool.Fori(1, PAIRS // 2) as i:
                for c in range(2):
                    gather(*pair(i, c), reuse=True)

        @block.tensor
        def _(pe):
            def embeddings(p, par, use):
                n = 0
                for k in range(NO):
                    if k % 2 == 0:
                        if not (isinstance(p, int) and p * EMB_BATCHES + n < EMB_BANKS):
                            pe.wait_ge(emb_ps_empty, p * EMB_BATCHES + n + 1 - EMB_BANKS)
                        bank = emb_ps[n % EMB_BANKS]
                        n += 1
                    pe.wait_ge(onehot_ready, p * NO + k + 1)
                    dst = bank[:, (k % 2) * PAIR:(k % 2 + 1) * PAIR]
                    for j in range(ROWS_PER):
                        for part, table in enumerate((table_hi, table_lo)):
                            last = nc.tensor.matmul(dst, table[0:ROWS, k, j, :],
                                                    onehot[0:ROWS, k % ONEHOT_RING, j, :],
                                                    start=(j == 0 and part == 0),
                                                    stop=(j == ROWS_PER - 1 and part == 1))
                    if k % 2 == 1 or k == NO - 1:
                        last.then_inc(emb_ps_full, 1)
                for t in range(TILES):
                    slot = par * TILES + t
                    pe.wait_ge(gathered[slot], (use + 1) * (16 * NG))
                    first = 0
                    for size in TR_SIZES:
                        if not (isinstance(p, int) and p * EMB_BATCHES + n < EMB_BANKS):
                            pe.wait_ge(emb_ps_empty, p * EMB_BATCHES + n + 1 - EMB_BANKS)
                        for f in range(size):
                            last = nc.tensor.transpose(emb_ps[n % EMB_BANKS][:, f * P:(f + 1) * P],
                                                       rows[:, slot, first + f, :], ident[:])
                        last.then_inc(emb_ps_full, 1)
                        first += size
                        n += 1

            def gram_products(p):
                pe.wait_ge(emb_ps_empty, (p + 1) * EMB_BATCHES)
                for a in range(GRAM_BATCHES):
                    if not (isinstance(p, int) and p * GRAM_BATCHES + a < GRAM_BANKS):
                        pe.wait_ge(gram_ps_empty, p * GRAM_BATCHES + a + 1 - GRAM_BANKS)
                    for b in range(PER_BANK):
                        t, g = divmod(a * PER_BANK + b, P // NQ)
                        samples = emb[:, t, g * NQ:(g + 1) * NQ, :]
                        last = nc.tensor.matmul(gram_ps[a % GRAM_BANKS][:, b * GCOLS:(b + 1) * GCOLS],
                                                samples.rearrange("d b s -> d (b s)"), samples[:, :, 0:NF], start=True, stop=True)
                    last.then_inc(gram_ps_full, 1)

            def mlp(p, par, use):
                pe.wait_ge(folded_dve, (p + 1) * NR)
                pe.wait_ge(folded_act, (p + 1) * NR)
                pe.wait_ge(dense_loaded[par], (use + 1) * 16)
                base = p * MLP_CHUNKS
                for m in range(M1):
                    if m > 1:
                        pe.wait_ge(mlp_empty, base + m - 1)
                    elif m == 0 and not (isinstance(p, int) and p == 0):
                        pe.wait_ge(mlp_empty, base)
                    for s in range(STEPS):
                        last = nc.tensor.matmul(mlp_ps[m % 2][:, 0:PAIR], w1_sb[:, s, m * P:(m + 1) * P],
                                                folded[:, par, s, :], start=(s == 0), stop=(s == STEPS - 1))
                    last.then_inc(mlp_full, 1)
                pe.wait_ge(mlp_empty, base + M1)
                for m in range(M2):
                    for k in range(M1):
                        last = nc.tensor.matmul(mlp_ps[(M1 + m) % 2][:, 0:PAIR], w2_sb[:, k, m * P:(m + 1) * P],
                                                h1[:, k, :], start=(k == 0), stop=(k == M1 - 1))
                    last.then_inc(mlp_full, 1)
                pe.wait_ge(mlp_empty, base + M1 + M2)
                for k in range(M2):
                    last = nc.tensor.matmul(mlp_ps[(M1 + M2) % 2][0:1, 0:PAIR], w3_sb[:, k:k + 1],
                                            h2[:, k, :], start=(k == 0), stop=(k == M2 - 1))
                last.then_inc(mlp_full, 1)

            pe.wait_ge(split_steps, 2 * NO)
            pe.wait_ge(ident_steps, 3)
            pe.wait_ge(weights_loaded, 5 * 16)
            pe.wait_ge(cleared, 3)
            embeddings(*pair(0, 0))
            gram_products(0)
            embeddings(*pair(0, 1))
            with pe.Fori(0, PAIRS // 2 - 1) as i:
                for c in range(1, 3):
                    gram_products(pair(i, c)[0])
                    mlp(*pair(i, c - 1))
                    embeddings(*pair(i, c + 1))
            gram_products(PAIRS - 1)
            mlp(*pair(0, PAIRS - 2))
            mlp(*pair(0, PAIRS - 1))

        @block.vector
        def _(dve):
            def make_onehots(p, par, use, tables):
                dve.wait_ge(ids_b_loaded[par], (use + 1) * 16)
                for k in tables:
                    slot = k % ONEHOT_RING
                    if k >= ONEHOT_RING:
                        dve.wait_ge(emb_ps_full, p * EMB_BATCHES + (k - ONEHOT_RING) // 2 + 1)
                    elif not (isinstance(p, int) and p == 0):
                        before = max(range(slot, NO, ONEHOT_RING))
                        dve.wait_ge(emb_ps_full, (p - 1) * EMB_BATCHES + before // 2 + 1)
                    for j in range(ROWS_PER):
                        last = nc.vector.tensor_scalar(onehot[0:ROWS, slot, j, :], ids_b[0:ROWS, par, k, :],
                                                       row_id[0:ROWS, j:j + 1], None, ALU.is_equal)
                    last.then_inc(onehot_ready, 1)

            def fold(p, par):
                dve.wait_ge(gram_ps_empty, (p + 1) * GRAM_BATCHES)
                for r, copies in enumerate(ROUNDS):
                    if r:
                        dve.wait_ge(folded_dve, p * NR + r)
                    for q in FOLD_DVE:
                        for copy in copies:
                            dst, src = fold_aps(par, q, copy)
                            last = nc.vector.tensor_copy(dst, src)
                    last.then_inc(folded_dve, 1)

            nc.vector.memset(folded[:], 0.0).then_inc(cleared, 1)
            dve.wait_ge(ident_steps, 2)
            nc.vector.tensor_copy(row_id[:], row_id_i[:]).then_inc(cleared, 1)
            for n in range(NO):
                whole = stage[0:ROWS, n * ROWS_PER * DIM:(n + 1) * ROWS_PER * DIM]
                hi = table_hi[0:ROWS, n, :, :].rearrange("p j d -> p (j d)")
                dve.wait_ge(table_loaded[n], 16)
                nc.vector.tensor_copy(hi, whole).then_inc(split_steps, 1)
                dve.wait_ge(split_steps, 2 * n + 1)
                nc.vector.tensor_tensor(table_lo[0:ROWS, n, :, :].rearrange("p j d -> p (j d)"),
                                        whole, hi.bitcast(F32), ALU.subtract).then_inc(split_steps, 1)
            dve.wait_ge(split_steps, 2 * NO)
            nc.vector.memset(emb[:, :, :, NF:QUAD], 0.0).then_inc(cleared, 1)
            dve.wait_ge(cleared, 3)
            make_onehots(*pair(0, 0), range(NO))
            make_onehots(*pair(0, 1), range(min(NO, ONEHOT_RING)))
            fold(0, 0)
            make_onehots(*pair(0, 1), range(ONEHOT_RING, NO))
            with dve.Fori(0, PAIRS // 2 - 1) as i:
                for c in range(1, 3):
                    p, par, _ = pair(i, c)
                    make_onehots(*pair(i, c + 1), range(min(NO, ONEHOT_RING)))
                    fold(p, par)
                    make_onehots(*pair(i, c + 1), range(ONEHOT_RING, NO))
            fold(PAIRS - 1, (PAIRS - 1) % 2)

        @block.scalar
        def _(act):
            def take_embeddings(p):
                n = 0
                first = NG
                for size in OH_SIZES:
                    act.wait_ge(emb_ps_full, p * EMB_BATCHES + n + 1)
                    nc.scalar.copy(emb[:, :, :, first:first + size],
                                   emb_ps[n % EMB_BANKS][:, 0:size * PAIR].rearrange(
                                       "d (f t b) -> d t b f", f=size, t=TILES)).then_inc(emb_ps_empty, 1)
                    first += size
                    n += 1
                for t in range(TILES):
                    first = 0
                    for size in TR_SIZES:
                        act.wait_ge(emb_ps_full, p * EMB_BATCHES + n + 1)
                        nc.scalar.copy(emb[:, t, :, first:first + size],
                                       emb_ps[n % EMB_BANKS][:, 0:size * P].rearrange(
                                           "d (f b) -> d b f", f=size)).then_inc(emb_ps_empty, 1)
                        first += size
                        n += 1

            def take_gram(p):
                if not (isinstance(p, int) and p == 0):
                    act.wait_ge(folded_dve, p * NR)
                    act.wait_ge(folded_act, p * NR)
                for a in range(GRAM_BATCHES):
                    act.wait_ge(gram_ps_full, p * GRAM_BATCHES + a + 1)
                    nc.scalar.copy(gram[:, a, :], gram_ps[a % GRAM_BANKS][:, 0:PER_BANK * GCOLS]
                                   ).then_inc(gram_ps_empty, 1)

            def take_mlp(p, par, use, c):
                src = mlp_ps[c % 2]
                act.wait_ge(mlp_full, p * MLP_CHUNKS + c + 1)
                if c < M1:
                    nc.scalar.activation(h1[:, c, :], src[:, 0:PAIR], ACT.Relu,
                                         bias=b1_sb[:, c:c + 1]).then_inc(mlp_empty, 1)
                elif c < M1 + M2:
                    nc.scalar.activation(h2[:, c - M1, :], src[:, 0:PAIR], ACT.Relu,
                                         bias=b2_sb[:, c - M1:c - M1 + 1]).then_inc(mlp_empty, 1)
                else:
                    if not (isinstance(use, int) and use == 0):
                        act.wait_ge(y_stored[par], use * 16)
                    nc.scalar.copy(y[:, par, :], src[0:1, 0:PAIR]).then_inc(mlp_empty, 1)

            def fold_and_mlp(p, par, before):
                chunk = 0
                act.wait_ge(gram_ps_empty, (p + 1) * GRAM_BATCHES)
                done = 0
                total = NR * len(FOLD_ACT) * len(ROUNDS[0])
                for r, copies in enumerate(ROUNDS):
                    if r:
                        act.wait_ge(folded_act, p * NR + r)
                    for q in FOLD_ACT:
                        for copy in copies:
                            dst, src = fold_aps(par, q, copy)
                            last = nc.scalar.copy(dst, src)
                            done += 1
                            if before is not None and done * MLP_CHUNKS // total > chunk and \
                                    (q, copy) != (FOLD_ACT[-1], copies[-1]):
                                take_mlp(*before, chunk)
                                chunk += 1
                    last.then_inc(folded_act, 1)
                if before is not None:
                    for c in range(chunk, MLP_CHUNKS):
                        take_mlp(*before, c)

            act.wait_ge(weights_loaded, 5 * 16)
            act.wait_ge(cleared, 3)
            take_embeddings(0)
            take_gram(0)
            fold_and_mlp(0, 0, None)
            take_embeddings(1)
            with act.Fori(0, PAIRS // 2 - 1) as i:
                for c in range(1, 3):
                    p, par, _ = pair(i, c)
                    take_gram(p)
                    fold_and_mlp(p, par, pair(i, c - 1))
                    take_embeddings(p + 1)
            take_gram(PAIRS - 1)
            fold_and_mlp(PAIRS - 1, (PAIRS - 1) % 2, pair(0, PAIRS - 2))
            for c in range(MLP_CHUNKS):
                take_mlp(*pair(0, PAIRS - 1), c)



def layer1_layout(w):
    laid = np.zeros((STEPS, P, HID1), w.dtype)
    for c, row, other in folded_pairs():
        i, j = sorted((SLOT_FEATURE[row], SLOT_FEATURE[other]))
        n = i * NF - i * (i + 1) // 2 + (j - i - 1)
        laid[c // NQ, (c % NQ) * QUAD + row] = w[n]
    q = DENSE_COLUMN % NQ
    laid[DENSE_COLUMN // NQ, q * QUAD:q * QUAD + DENSE] = w[NF * (NF - 1) // 2:]
    return laid.transpose(1, 0, 2)


def kernel(**inputs):
    import concourse.bacc as bacc
    from concourse.bass_utils import run_bass_kernel_spmd

    a = {k: np.asarray(v) for k, v in inputs.items()}
    ids = a["ids"]
    nc = bacc.Bacc("TRN2", target_bir_lowering=False, num_devices=1)
    arrays = {}

    def dram(name, array):
        arrays[name] = np.ascontiguousarray(array)
        return nc.dram_tensor(name, arrays[name].shape, mybir.dt.from_np(arrays[name].dtype),
                              kind="ExternalInput").ap()

    out = nc.dram_tensor("out", (BATCH, 1), F32, kind="ExternalOutput").ap()
    build(
        nc,
        dram("dense_t", a["dense_ctx"].T),
        dram("ids_rows", ids[:, GATHERED].reshape(BATCH // P, P, NG)),
        dram("ids_onehot", ids[:, ONEHOT].T),
        [dram(f"tbl_{f}_rows", a[f"tbl_{f}"]) for f in GATHERED],
        [dram(f"tbl_{f}_rows", a[f"tbl_{f}"]) for f in ONEHOT],
        dram("w1", layer1_layout(a["W_top1"])),
        dram("w2", a["W_top2"].reshape(M1, P, HID2).transpose(1, 0, 2)),
        dram("w3", a["W_top3"].reshape(M2, P).T),
        dram("b1", a["b_top1"].reshape(M1, P).T),
        dram("b2", a["b_top2"].reshape(M2, P).T),
        out,
    )
    r = run_bass_kernel_spmd(nc, [arrays], core_ids=[0])
    return r.results[0]["out"]
```

```python
from contextlib import ExitStack

import numpy as np

import concourse.bass as bass
from concourse import mybir

F32 = mybir.dt.float32
F32R = mybir.dt.float32r
I32 = mybir.dt.int32
ALU = mybir.AluOpType
ACT = mybir.ActivationFunctionType

P = 128
QUAD = 32
NQ = P // QUAD
BATCH = 2048
NF = 27
DIM = 128
DENSE = 16
HID1, HID2 = 512, 256
TILES = 2
PAIR = TILES * P
PAIRS = BATCH // PAIR

VOCAB_ONEHOT = 1000
ROWS = 125
ROWS_PER = VOCAB_ONEHOT // ROWS
ONEHOT = [3, 5, 7, 8, 11, 13, 14]
GATHERED = [f for f in range(NF) if f not in ONEHOT]
NG, NO = len(GATHERED), len(ONEHOT)
SLOT_FEATURE = GATHERED + ONEHOT

GROUP = NF // 3
BETWEEN, WITHIN = GROUP, GROUP - 1
STEPS = -(-(BETWEEN + WITHIN + 1) // NQ)
DENSE_COLUMN = BETWEEN + WITHIN

GRAMS = PAIR // NQ
PER_BANK = 4
GRAM_BATCHES = GRAMS // PER_BANK
GRAM_BANKS = 2
GCOLS = NQ * NF
TR_PER_BANK = 4
EMB_BANKS = 3
M1, M2 = HID1 // P, HID2 // P
MLP_CHUNKS = M1 + M2 + 1
ONEHOT_RING = 4
FOLD_DVE = 2


def emb_order(spread):
    lookups = [(None, k, 1) for k in range(NO)]
    turned = [[(t, f, min(TR_PER_BANK, NG - f)) for f in range(0, NG, TR_PER_BANK)] for t in range(TILES)]
    if not spread:
        return lookups + turned[0] + turned[1]
    order = []
    while len(turned[0]) > 1:
        per = -(-len(lookups) // (len(turned[0]) - 1))
        order += lookups[:per] + turned[0][:1]
        del lookups[:per], turned[0][:1]
    return order + turned[0] + turned[1]


EMB_ORDER = emb_order(True)
FIRST_ORDER = emb_order(False)
EMB_BATCHES = len(EMB_ORDER)
EMB_FIRST = EMB_BATCHES - -(-NG // TR_PER_BANK)


def before(n, banks, batches):
    return n - banks + 1 if n >= banks else max(range(n, batches, banks)) + 1 - batches


def order_of(p):
    return FIRST_ORDER if isinstance(p, int) and p < 2 else EMB_ORDER


def banks_until_looked_up(p, k):
    return 1 + order_of(p).index((None, k, 1))


def banks_until_transposed(tile):
    first, later = (1 + max(n for n, (t, _, _) in enumerate(order) if t == tile)
                    for order in (FIRST_ORDER, EMB_ORDER))
    assert first == later
    return later


def fold_copies():
    rounds = []
    for rows, between, within in ((3, 0, 2), (2, 2, 1), (1, 1, 0)):
        copies = []
        for first, count, group in ((0, BETWEEN, between), (BETWEEN, WITHIN, within)):
            for k in range(NQ):
                n = len(range(k, count, NQ))
                quad, step = (first + k) % NQ, (first + k) // NQ
                copies.append((quad, step, n, rows * GROUP, group * GROUP + k))
        rounds.append(copies)
    return rounds


def folded_pairs():
    seen, out = set(), []
    for c in range(BETWEEN + WITHIN):
        for row in range(NF):
            g = row // GROUP
            other = ((g + 1) % 3) * GROUP + c if c < BETWEEN else g * GROUP + c - BETWEEN
            pair = frozenset((row, other))
            if row != other and pair not in seen:
                seen.add(pair)
                out.append((c, row, other))
    assert len(out) == NF * (NF - 1) // 2
    return out


def build(nc, dense_t, ids_rows, ids_onehot, gathered_tables, onehot_tables, w1, w2, w3, b1, b2, out):
    with ExitStack() as ctx:
        def sb(name, shape, dt=F32):
            return ctx.enter_context(nc.sbuf_tensor(name, shape, dt))

        def sem(name):
            return ctx.enter_context(nc.semaphore(name))

        idx = sb("idx", [P, 2, TILES * NG], I32)
        ids_b = sb("ids_b", [P, NO, PAIR], I32)
        rows = sb("rows", [P, TILES, NG, DIM])
        emb = sb("emb", [P, TILES, P, QUAD])
        gram = sb("gram", [P, GRAM_BATCHES, PER_BANK * GCOLS])
        folded = sb("folded", [P, 2, STEPS, PAIR])
        table_hi = sb("table_hi", [P, NO, ROWS_PER, DIM], F32R)
        table_lo = sb("table_lo", [P, NO, ROWS_PER, DIM], F32R)
        onehot = sb("onehot", [P, ONEHOT_RING, ROWS_PER, PAIR], F32R)
        row_id_i = sb("row_id_i", [P, ROWS_PER], I32)
        ident = sb("ident", [P, P])
        w1_sb = sb("w1_sb", [P, STEPS, HID1])
        w2_sb = sb("w2_sb", [P, M1, HID2])
        w3_sb = sb("w3_sb", [P, M2])
        b1_sb = sb("b1_sb", [P, M1])
        b2_sb = sb("b2_sb", [P, M2])
        h1 = sb("h1", [P, M1, PAIR])
        h2 = sb("h2", [P, M2, PAIR])
        y = sb("y", [1, 2, PAIR])
        spaces = [gram[:, :, :].rearrange("p a b -> p (a b)"), folded[:, :, :, :].rearrange("p a b c -> p (a b c)")]
        part = ROWS_PER * DIM
        stages = [space[0:ROWS, k:k + part] for space in spaces for k in range(0, space.shape[1] - part + 1, part)]

        gram_ps = [ctx.enter_context(nc.psum_tensor(f"gram_ps{i}", [P, 512], F32)) for i in range(GRAM_BANKS)]
        emb_ps = [ctx.enter_context(nc.psum_tensor(f"emb_ps{i}", [P, 512], F32)) for i in range(EMB_BANKS)]
        row_id = ctx.enter_context(nc.psum_tensor("row_id", [P, 512], F32))
        mlp_ps = [ctx.enter_context(nc.psum_tensor(f"mlp_ps{i}", [P, 512], F32)) for i in range(2)]

        idx_loaded = [sem(f"idx_loaded{i}") for i in range(2)]
        ids_b_loaded = sem("ids_b_loaded")
        dense_loaded = [sem(f"dense_loaded{i}") for i in range(2)]
        table_loaded = [sem(f"table_loaded{i}") for i in range(NO)]
        weights_loaded = sem("weights_loaded")
        gathered = [sem(f"gathered{i}") for i in range(TILES)]
        gather_begun = sem("gather_begun")
        ident_steps = sem("ident_steps")
        table_rounded = sem("table_rounded")
        table_split = sem("table_split")
        cleared = sem("cleared")
        onehot_ready = sem("onehot_ready")
        emb_ps_full = sem("emb_ps_full")
        emb_ps_empty = sem("emb_ps_empty")
        gram_ps_full = sem("gram_ps_full")
        gram_ps_empty = sem("gram_ps_empty")
        folded_dve = sem("folded_dve")
        folded_act = sem("folded_act")
        mlp_full = sem("mlp_full")
        mlp_empty = sem("mlp_empty")
        y_stored = [sem(f"y_stored{i}") for i in range(2)]

        ROUNDS = fold_copies()
        NR = len(ROUNDS)
        LAST = PAIRS - 1
        LAST_MLP_CHUNKS = MLP_CHUNKS + M1
        BOTH = (0, TILES)

        def pair(i, c):
            return i * 2 + c, i + c // 2

        def rounds_before(p):
            return p * TILES * NR if isinstance(p, int) and p < 2 else (p + 2) * NR

        def tile_share(p, t):
            return NQ - 1 if t == 0 or p == LAST else FOLD_DVE

        def fold_aps(par, q, copy, t0, t1):
            quad, step, n, nrows, src = copy
            dst = folded[quad * QUAD:quad * QUAD + nrows, par, step:step + n, t0 * P:t1 * P].rearrange(
                "p n (b q) -> p n b q", q=NQ)[:, :, :, q]
            col = q * NF + src
            batches = GRAM_BATCHES // TILES
            products = gram[q * QUAD:q * QUAD + nrows, t0 * batches:t1 * batches, :].rearrange(
                "p a (b c) -> p c (a b)", c=GCOLS)
            return dst, products[:, col:col + NQ * (n - 1) + 1:NQ, :]

        block = ctx.enter_context(nc.Block())

        @block.sync
        def _(sp):
            def load_idx(p, par):
                for t in range(TILES):
                    sp.dma_start(idx[:, par, t * NG:(t + 1) * NG],
                                 ids_rows[bass.ds(p * TILES + t, 1), :, :].rearrange("o p f -> (o p) f")
                                 ).then_inc(idx_loaded[par], 16)

            def load_ids_b(p):
                sp.dma_start(ids_b[:], ids_onehot[:, bass.ds(p * PAIR, PAIR)].partition_broadcast(P)
                             ).then_inc(ids_b_loaded, 16)

            def load_dense(p, par):
                q, step = DENSE_COLUMN % NQ, DENSE_COLUMN // NQ
                sp.dma_start(folded[q * QUAD:q * QUAD + DENSE, par, step, :],
                             dense_t[:, bass.ds(p * PAIR, PAIR)]).then_inc(dense_loaded[par], 16)

            def next_ids_b(p):
                sp.wait_ge(onehot_ready, (p + 1) * NO)
                load_ids_b(p + 1)

            def next_idx(p, par):
                for t in range(TILES):
                    sp.wait_ge(gathered[t], (p + 1) * (16 * NG))
                load_idx(p + 2, par)

            def next_dense(p, par):
                sp.wait_ge(mlp_full, p * MLP_CHUNKS + M1)
                load_dense(p + 2, par)

            def store_y(p, par, chunks):
                sp.wait_ge(mlp_empty, p * MLP_CHUNKS + chunks)
                sp.dma_start(out[bass.ds(p * PAIR, PAIR), :].rearrange("n o -> o n"),
                             y[:, par, :]).then_inc(y_stored[par], 16)

            load_idx(0, 0)
            for n in range(NO):
                sp.dma_start(stages[n], onehot_tables[n].rearrange("(p j) d -> p (j d)", j=ROWS_PER)
                             ).then_inc(table_loaded[n], 16)
                if n == 0:
                    load_ids_b(0)
            load_idx(1, 1)
            for dst, src in ((w1_sb, w1), (w2_sb, w2), (w3_sb, w3), (b1_sb, b1), (b2_sb, b2)):
                sp.dma_start(dst[:], src).then_inc(weights_loaded, 16)
            sp.wait_ge(cleared, 3)
            load_dense(0, 0)
            load_dense(1, 1)
            next_ids_b(0)
            next_idx(0, 0)
            next_ids_b(1)
            next_idx(1, 1)
            next_dense(0, 0)
            with sp.Fori(1, PAIRS // 2 - 1) as i:
                for c in range(2):
                    p, _ = pair(i, c)
                    next_ids_b(p)
                    next_idx(p, c)
                    store_y(p - 2, c, MLP_CHUNKS)
                    next_dense(p - 1, (c - 1) % 2)
            next_ids_b(LAST - 1)
            store_y(LAST - 3, (LAST - 3) % 2, MLP_CHUNKS)
            next_dense(LAST - 2, (LAST - 2) % 2)
            store_y(LAST - 2, (LAST - 2) % 2, MLP_CHUNKS)
            store_y(LAST - 1, (LAST - 1) % 2, MLP_CHUNKS)
            store_y(LAST, LAST % 2, LAST_MLP_CHUNKS)
            for par in range(2):
                sp.wait_ge(y_stored[par], 16 * (PAIRS // 2))

        @block.gpsimd
        def _(pool):
            def gather(p, par, use):
                for t in range(TILES):
                    pool.wait_ge(idx_loaded[par], (use + 1) * (16 * TILES))
                    if not (isinstance(p, int) and p == 0):
                        pool.wait_ge(emb_ps_full, (p - 1) * EMB_BATCHES + banks_until_transposed(t))
                    pool.sem_inc(gather_begun, 1)
                    for n in range(NG):
                        col = t * NG + n
                        pool.indirect_dma_start(
                            out=rows[:, t, n, :], out_offset=None, in_=gathered_tables[n],
                            in_offset=bass.IndirectOffsetOnAxis(ap=idx[:, par, col:col + 1], axis=0),
                        ).then_inc(gathered[t], 16)

            nc.gpsimd.memset(ident[:], 0.0).then_inc(ident_steps, 1)
            nc.gpsimd.iota(row_id_i[:], pattern=[[1, ROWS_PER]], base=0,
                           channel_multiplier=ROWS_PER).then_inc(ident_steps, 1)
            pool.wait_ge(ident_steps, 2)
            nc.gpsimd.affine_select(out=ident[:], in_=ident[:], compare_op=ALU.not_equal, fill=1.0,
                                    base=0, pattern=[[-1, P]], channel_multiplier=1).then_inc(ident_steps, 1)
            gather(0, 0, 0)
            with pool.Fori(0, PAIRS // 2 - 1) as i:
                for c in range(1, 3):
                    p, use = pair(i, c)
                    gather(p, c % 2, use)
            gather(LAST, LAST % 2, LAST // 2)

        @block.tensor
        def _(pe):
            def embeddings(p, n0, n1):
                for n in range(n0, n1):
                    t, first, size = order_of(p)[n]
                    bank = emb_ps[n % EMB_BANKS]
                    if not (isinstance(p, int) and p == 0 and n < EMB_BANKS):
                        pe.wait_ge(emb_ps_empty, p * EMB_BATCHES + before(n, EMB_BANKS, EMB_BATCHES))
                    if t is None:
                        pe.wait_ge(onehot_ready, p * NO + first + 1)
                        for j in range(ROWS_PER):
                            for part, table in enumerate((table_hi, table_lo)):
                                last = nc.tensor.matmul(bank[:, 0:PAIR], table[0:ROWS, first, j, :],
                                                        onehot[0:ROWS, first % ONEHOT_RING, j, :],
                                                        start=(j == 0 and part == 0),
                                                        stop=(j == ROWS_PER - 1 and part == 1))
                    else:
                        if first == 0:
                            pe.wait_ge(gathered[t], (p + 1) * (16 * NG))
                        for f in range(size):
                            last = nc.tensor.transpose(bank[:, f * P:(f + 1) * P],
                                                       rows[:, t, first + f, :], ident[:])
                    last.then_inc(emb_ps_full, 1)

            def gram_products(p, t0, t1, banks):
                pe.wait_ge(emb_ps_empty, p * EMB_BATCHES + banks)
                for a in range(t0 * GRAM_BATCHES // TILES, t1 * GRAM_BATCHES // TILES):
                    if not (isinstance(p, int) and p == 0 and a < GRAM_BANKS):
                        pe.wait_ge(gram_ps_empty, p * GRAM_BATCHES + before(a, GRAM_BANKS, GRAM_BATCHES))
                    for b in range(PER_BANK):
                        t, g = divmod(a * PER_BANK + b, P // NQ)
                        samples = emb[:, t, g * NQ:(g + 1) * NQ, :]
                        last = nc.tensor.matmul(gram_ps[a % GRAM_BANKS][:, b * GCOLS:(b + 1) * GCOLS],
                                                samples.rearrange("d b s -> d (b s)"),
                                                samples[:, :, 0:NF], start=True, stop=True)
                    last.then_inc(gram_ps_full, 1)

            def layer1(par, t0, t1, chunks, odd, rounds, loads):
                pe.wait_ge(folded_dve, rounds)
                pe.wait_ge(folded_act, rounds)
                pe.wait_ge(dense_loaded[par], loads * 16)
                c0, c1 = t0 * P, t1 * P
                for m in range(M1):
                    if not (isinstance(chunks, int) and chunks + m < 2):
                        pe.wait_ge(mlp_empty, chunks + m - 1)
                    for s in range(STEPS):
                        last = nc.tensor.matmul(mlp_ps[(odd + m) % 2][:, c0:c1], w1_sb[:, s, m * P:(m + 1) * P],
                                                folded[:, par, s, c0:c1], start=(s == 0), stop=(s == STEPS - 1))
                    last.then_inc(mlp_full, 1)

            def layer2(chunks, odd):
                pe.wait_ge(mlp_empty, chunks)
                for m in range(M2):
                    for k in range(M1):
                        last = nc.tensor.matmul(mlp_ps[(odd + m) % 2][:, 0:PAIR], w2_sb[:, k, m * P:(m + 1) * P],
                                                h1[:, k, :], start=(k == 0), stop=(k == M1 - 1))
                    last.then_inc(mlp_full, 1)

            def layer3(chunks, odd):
                pe.wait_ge(mlp_empty, chunks)
                for k in range(M2):
                    last = nc.tensor.matmul(mlp_ps[odd % 2][0:1, 0:PAIR], w3_sb[:, k:k + 1],
                                            h2[:, k, :], start=(k == 0), stop=(k == M2 - 1))
                last.then_inc(mlp_full, 1)

            def layer1_of_pair(p, use, par):
                layer1(par, *BOTH, p * MLP_CHUNKS, par * MLP_CHUNKS, rounds_before(p + 1), use + 1)

            def layer2_of_pair(p, par):
                layer2(p * MLP_CHUNKS + M1, par * MLP_CHUNKS + M1)

            def layer3_of_pair(p, par):
                layer3(p * MLP_CHUNKS + M1 + M2, par * MLP_CHUNKS + M1 + M2)

            pe.wait_ge(ident_steps, 3)
            pe.wait_ge(cleared, 1)
            embeddings(0, 0, EMB_FIRST)
            gram_products(0, 0, 1, EMB_FIRST)
            embeddings(0, EMB_FIRST, EMB_BATCHES)
            gram_products(0, 1, 2, EMB_BATCHES)
            embeddings(1, 0, EMB_FIRST)
            pe.wait_ge(weights_loaded, 5 * 16)
            layer1_of_pair(0, 0, 0)
            gram_products(1, 0, 1, EMB_FIRST)
            layer2_of_pair(0, 0)
            embeddings(1, EMB_FIRST, EMB_BATCHES)
            gram_products(1, 1, 2, EMB_BATCHES)
            embeddings(2, 0, EMB_BATCHES)
            with pe.Fori(1, PAIRS // 2 - 1) as i:
                for c in range(2):
                    p, _ = pair(i, c)
                    gram_products(p, *BOTH, EMB_BATCHES)
                    layer3_of_pair(p - 2, c)
                    layer1_of_pair(*pair(i, c - 1), (c - 1) % 2)
                    embeddings(p + 1, 0, EMB_BATCHES)
                    layer2_of_pair(p - 1, (c - 1) % 2)
            p = LAST - 1
            gram_products(p, *BOTH, EMB_BATCHES)
            layer3_of_pair(p - 2, p % 2)
            layer1_of_pair(p - 1, (p - 1) // 2, (p - 1) % 2)
            embeddings(LAST, 0, EMB_FIRST)
            layer2_of_pair(p - 1, (p - 1) % 2)
            gram_products(LAST, 0, 1, EMB_FIRST)
            layer3_of_pair(p - 1, (p - 1) % 2)
            layer1_of_pair(p, p // 2, p % 2)
            embeddings(LAST, EMB_FIRST, EMB_BATCHES)
            gram_products(LAST, 1, 2, EMB_BATCHES)
            layer2_of_pair(p, p % 2)
            layer3_of_pair(p, p % 2)
            for t in range(TILES):
                chunks = LAST * MLP_CHUNKS + t * M1
                layer1(LAST % 2, t, t + 1, chunks, chunks, rounds_before(LAST) + (t + 1) * NR, PAIRS // 2)
            chunks = LAST * MLP_CHUNKS + TILES * M1
            layer2(chunks, chunks)
            layer3(chunks + M2, chunks + M2)

        @block.vector
        def _(dve):
            def make_onehots(p, tables):
                dve.wait_ge(ids_b_loaded, (p + 1) * 16)
                for k in tables:
                    slot = k % ONEHOT_RING
                    if k >= ONEHOT_RING:
                        dve.wait_ge(emb_ps_full, p * EMB_BATCHES + banks_until_looked_up(p, k - ONEHOT_RING))
                    elif not (isinstance(p, int) and p == 0):
                        user = max(range(slot, NO, ONEHOT_RING))
                        dve.wait_ge(emb_ps_full, (p - 1) * EMB_BATCHES + banks_until_looked_up(p - 1, user))
                    nc.vector.tensor_tensor(
                        onehot[0:ROWS, slot, :, :],
                        ids_b[0:ROWS, k, :].unsqueeze(1).broadcast_to([ROWS, ROWS_PER, PAIR]),
                        row_id[0:ROWS, 0:ROWS_PER].unsqueeze(2).broadcast_to([ROWS, ROWS_PER, PAIR]),
                        ALU.is_equal).then_inc(onehot_ready, 1)

            def fold(par, t0, t1, batches, rounds, share=FOLD_DVE):
                dve.wait_ge(gram_ps_empty, batches)
                for r, copies in enumerate(ROUNDS):
                    if r:
                        dve.wait_ge(folded_dve, rounds + r)
                    for q in range(share):
                        for copy in copies:
                            dst, src = fold_aps(par, q, copy, t0, t1)
                            last = nc.vector.tensor_copy(dst, src)
                    last.then_inc(folded_dve, 1)

            def fold_pair(p, par):
                fold(par, *BOTH, (p + 1) * GRAM_BATCHES, rounds_before(p))

            def fold_tile(p, par, t):
                fold(par, t, t + 1, p * GRAM_BATCHES + (t + 1) * GRAM_BATCHES // TILES,
                     rounds_before(p) + t * NR, tile_share(p, t))

            nc.vector.memset(emb[:, :, :, NF:QUAD], 0.0).then_inc(cleared, 1)
            dve.wait_ge(ident_steps, 2)
            nc.vector.tensor_copy(row_id[:, 0:ROWS_PER], row_id_i[:]).then_inc(cleared, 1)
            dve.wait_ge(cleared, 2)
            for n in range(NO):
                dve.wait_ge(table_loaded[n], 16)
                dve.wait_ge(table_rounded, n + 1)
                nc.vector.tensor_tensor(table_lo[0:ROWS, n, :, :].rearrange("p j d -> p (j d)"), stages[n],
                                        table_hi[0:ROWS, n, :, :].rearrange("p j d -> p (j d)").bitcast(F32),
                                        ALU.subtract).then_inc(table_split, 1)
                make_onehots(0, [n])
            dve.wait_ge(table_split, NO)
            nc.vector.memset(folded[:], 0.0).then_inc(cleared, 1)
            dve.wait_ge(cleared, 3)
            make_onehots(1, range(ONEHOT_RING))
            for t in range(TILES):
                fold_tile(0, 0, t)
            make_onehots(1, range(ONEHOT_RING, NO))
            make_onehots(2, range(ONEHOT_RING))
            for t in range(TILES):
                fold_tile(1, 1, t)
            make_onehots(2, range(ONEHOT_RING, NO))
            with dve.Fori(1, PAIRS // 2 - 1) as i:
                for c in range(2):
                    p, _ = pair(i, c)
                    make_onehots(p + 1, range(ONEHOT_RING))
                    fold_pair(p, c)
                    make_onehots(p + 1, range(ONEHOT_RING, NO))
            make_onehots(LAST, range(ONEHOT_RING))
            fold_pair(LAST - 1, (LAST - 1) % 2)
            make_onehots(LAST, range(ONEHOT_RING, NO))
            for t in range(TILES):
                fold_tile(LAST, LAST % 2, t)

        @block.scalar
        def _(act):
            def take_bank(p, n):
                t, first, size = order_of(p)[n]
                bank = emb_ps[n % EMB_BANKS]
                act.wait_ge(emb_ps_full, p * EMB_BATCHES + n + 1)
                if t is None:
                    nc.scalar.copy(emb[:, :, :, NG + first], bank[:, 0:PAIR].rearrange("d (t b) -> d t b", t=TILES)
                                   ).then_inc(emb_ps_empty, 1)
                else:
                    nc.scalar.copy(emb[:, t, :, first:first + size],
                                   bank[:, 0:size * P].rearrange("d (f b) -> d b f", f=size)
                                   ).then_inc(emb_ps_empty, 1)

            def take_embeddings(p, n0, n1):
                for n in range(n0, n1):
                    take_bank(p, n)

            def take_gram(p, t0, t1):
                for a in range(t0 * GRAM_BATCHES // TILES, t1 * GRAM_BATCHES // TILES):
                    if a == 0 and not (isinstance(p, int) and p == 0):
                        act.wait_ge(folded_dve, rounds_before(p))
                        act.wait_ge(folded_act, rounds_before(p))
                    act.wait_ge(gram_ps_full, p * GRAM_BATCHES + a + 1)
                    nc.scalar.copy(gram[:, a, :], gram_ps[a % GRAM_BANKS][:, 0:PER_BANK * GCOLS]
                                   ).then_inc(gram_ps_empty, 1)

            def take_layer(layer, m, par, t0, t1, chunks, odd, stores=0):
                c0, c1 = t0 * P, t1 * P
                src = mlp_ps[odd % 2]
                act.wait_ge(mlp_full, chunks + 1)
                if layer == 1:
                    nc.scalar.activation(h1[:, m, c0:c1], src[:, c0:c1], ACT.Relu,
                                         bias=b1_sb[:, m:m + 1]).then_inc(mlp_empty, 1)
                elif layer == 2:
                    nc.scalar.activation(h2[:, m, c0:c1], src[:, c0:c1], ACT.Relu,
                                         bias=b2_sb[:, m:m + 1]).then_inc(mlp_empty, 1)
                else:
                    if not (isinstance(stores, int) and stores == 0):
                        act.wait_ge(y_stored[par], stores * 16)
                    nc.scalar.copy(y[:, par, c0:c1], src[0:1, c0:c1]).then_inc(mlp_empty, 1)

            def take_layer1(p, par, m):
                take_layer(1, m, par, *BOTH, p * MLP_CHUNKS + m, par * MLP_CHUNKS + m)

            def take_layer2_chunk(p, par, m):
                take_layer(2, m, par, *BOTH, p * MLP_CHUNKS + M1 + m, par * MLP_CHUNKS + M1 + m)

            def take_layer2(p, par):
                for m in range(M2):
                    take_layer2_chunk(p, par, m)

            def take_layer3(p, use, par):
                chunk = M1 + M2
                take_layer(3, 0, par, *BOTH, p * MLP_CHUNKS + chunk, par * MLP_CHUNKS + chunk, use)

            def fold(par, t0, t1, batches, rounds, between=0, take=None, share=FOLD_DVE):
                taken, done, total = 0, 0, NR * (NQ - share) * len(ROUNDS[0])
                act.wait_ge(gram_ps_empty, batches)
                for r, copies in enumerate(ROUNDS):
                    if r:
                        act.wait_ge(folded_act, rounds + r)
                    for q in range(share, NQ):
                        for copy in copies:
                            if done * (between + 1) // total > taken:
                                take(taken)
                                taken += 1
                            dst, src = fold_aps(par, q, copy, t0, t1)
                            last = nc.scalar.copy(dst, src)
                            done += 1
                    last.then_inc(folded_act, 1)
                for n in range(taken, between):
                    take(n)

            def fold_tile(p, par, t, between=0, take=None):
                fold(par, t, t + 1, p * GRAM_BATCHES + (t + 1) * GRAM_BATCHES // TILES,
                     rounds_before(p) + t * NR, between, take, tile_share(p, t))

            def fold_pair(p, par, before, before_par):
                fold(par, *BOTH, (p + 1) * GRAM_BATCHES, rounds_before(p), M1,
                     lambda m: take_layer1(before, before_par, m))

            for n in range(NO):
                act.wait_ge(table_loaded[n], 16)
                nc.scalar.copy(table_hi[0:ROWS, n, :, :].rearrange("p j d -> p (j d)"), stages[n]
                               ).then_inc(table_rounded, 1)
            act.wait_ge(cleared, 1)
            take_embeddings(0, 0, EMB_FIRST)
            act.wait_ge(table_split, NO)
            act.wait_ge(cleared, 3)
            take_gram(0, 0, 1)
            fold_tile(0, 0, 0, EMB_BATCHES - EMB_FIRST, lambda n: take_bank(0, EMB_FIRST + n))
            take_gram(0, 1, 2)
            fold_tile(0, 0, 1, ONEHOT_RING, lambda n: take_bank(1, n))
            take_embeddings(1, ONEHOT_RING, EMB_FIRST)
            act.wait_ge(weights_loaded, 5 * 16)
            for m in range(M1):
                take_layer1(0, 0, m)
            take_gram(1, 0, 1)
            fold_tile(1, 1, 0, M2 + EMB_BATCHES - EMB_FIRST,
                      lambda n: take_layer2_chunk(0, 0, n) if n < M2 else take_bank(1, EMB_FIRST + n - M2))
            take_gram(1, 1, 2)
            fold_tile(1, 1, 1, ONEHOT_RING, lambda n: take_bank(2, n))
            take_embeddings(2, ONEHOT_RING, EMB_BATCHES)
            with act.Fori(1, PAIRS // 2 - 1) as i:
                for c in range(2):
                    p, _ = pair(i, c)
                    take_gram(p, *BOTH)
                    take_layer3(*pair(i, c - 2), c)
                    fold_pair(p, c, p - 1, (c - 1) % 2)
                    take_embeddings(p + 1, 0, EMB_BATCHES)
                    take_layer2(p - 1, (c - 1) % 2)
            p = LAST - 1
            take_gram(p, *BOTH)
            take_layer3(p - 2, (p - 2) // 2, p % 2)
            fold_pair(p, p % 2, p - 1, (p - 1) % 2)
            take_embeddings(LAST, 0, EMB_FIRST)
            take_layer2(p - 1, (p - 1) % 2)
            par = LAST % 2

            def late_layers(n):
                if n < M2:
                    take_layer2_chunk(p, p % 2, n)
                else:
                    take_layer3(p, p // 2, p % 2)

            take_gram(LAST, 0, 1)
            take_layer3(p - 1, (p - 1) // 2, (p - 1) % 2)
            fold_tile(LAST, par, 0, M1, lambda m: take_layer1(p, p % 2, m))
            take_embeddings(LAST, EMB_FIRST, EMB_BATCHES)
            take_gram(LAST, 1, 2)
            fold_tile(LAST, par, 1, M2 + 1, late_layers)
            chunks = LAST * MLP_CHUNKS
            for t in range(TILES):
                for m in range(M1):
                    take_layer(1, m, par, t, t + 1, chunks, chunks)
                    chunks += 1
            for m in range(M2):
                take_layer(2, m, par, *BOTH, chunks, chunks)
                chunks += 1
            take_layer(3, 0, par, *BOTH, chunks, chunks, LAST // 2)



def layer1_layout(w):
    laid = np.zeros((STEPS, P, HID1), w.dtype)
    for c, row, other in folded_pairs():
        i, j = sorted((SLOT_FEATURE[row], SLOT_FEATURE[other]))
        n = i * NF - i * (i + 1) // 2 + (j - i - 1)
        laid[c // NQ, (c % NQ) * QUAD + row] = w[n]
    q = DENSE_COLUMN % NQ
    laid[DENSE_COLUMN // NQ, q * QUAD:q * QUAD + DENSE] = w[NF * (NF - 1) // 2:]
    return laid.transpose(1, 0, 2)


def kernel(**inputs):
    import concourse.bacc as bacc
    from concourse.bass_utils import run_bass_kernel_spmd

    a = {k: np.asarray(v) for k, v in inputs.items()}
    ids = a["ids"]
    nc = bacc.Bacc("TRN2", target_bir_lowering=False, num_devices=1)
    arrays = {}

    def dram(name, array):
        arrays[name] = np.ascontiguousarray(array)
        return nc.dram_tensor(name, arrays[name].shape, mybir.dt.from_np(arrays[name].dtype),
                              kind="ExternalInput").ap()

    out = nc.dram_tensor("out", (BATCH, 1), F32, kind="ExternalOutput").ap()
    build(
        nc,
        dram("dense_t", a["dense_ctx"].T),
        dram("ids_rows", ids[:, GATHERED].reshape(BATCH // P, P, NG)),
        dram("ids_onehot", ids[:, ONEHOT].T),
        [dram(f"tbl_{f}_rows", a[f"tbl_{f}"]) for f in GATHERED],
        [dram(f"tbl_{f}_rows", a[f"tbl_{f}"]) for f in ONEHOT],
        dram("w1", layer1_layout(a["W_top1"])),
        dram("w2", a["W_top2"].reshape(M1, P, HID2).transpose(1, 0, 2)),
        dram("w3", a["W_top3"].reshape(M2, P).T),
        dram("b1", a["b_top1"].reshape(M1, P).T),
        dram("b2", a["b_top2"].reshape(M2, P).T),
        out,
    )
    r = run_bass_kernel_spmd(nc, [arrays], core_ids=[0])
    return r.results[0]["out"]
```

```python
from contextlib import ExitStack

import numpy as np

import concourse.bass as bass
from concourse import mybir

F32 = mybir.dt.float32
F32R = mybir.dt.float32r
I32 = mybir.dt.int32
ALU = mybir.AluOpType
ACT = mybir.ActivationFunctionType

P = 128
QUAD = 32
NQ = P // QUAD
BATCH = 2048
NF = 27
DIM = 128
DENSE = 16
HID1, HID2 = 512, 256
TILES = 2
PAIR = TILES * P
PAIRS = BATCH // PAIR

VOCAB_ONEHOT = 1000
ROWS = 125
ROWS_PER = VOCAB_ONEHOT // ROWS
ONEHOT = [3, 5, 7, 8, 11, 13, 14]
GATHERED = [f for f in range(NF) if f not in ONEHOT]
NG, NO = len(GATHERED), len(ONEHOT)
SLOT_FEATURE = GATHERED + ONEHOT

GROUP = NF // 3
COLUMNS = 2 * GROUP
DENSE_COLUMN = COLUMNS
STEPS = -(-(COLUMNS + 1) // NQ)

GRAMS = PAIR // NQ
PER_BANK = 4
GRAM_BATCHES = GRAMS // PER_BANK
GRAM_BANKS = 2
GCOLS = NQ * NF
TR_PER_BANK = 4
EMB_BANKS = 3
M1, M2 = HID1 // P, HID2 // P
MLP_CHUNKS = M1 + M2 + 1
ONEHOT_RING = 4
TAKES_OF_FOLD = (6, 12, 18, 24, 25, 26, 31, 32, 37)


def emb_order(first_pairs):
    lookups = [(None, k, 1) for k in range(NO)]
    turned = [[(t, f, min(TR_PER_BANK, NG - f)) for f in range(0, NG, TR_PER_BANK)] for t in range(TILES)]
    if first_pairs:
        return lookups + turned[0] + turned[1]
    order = []
    while turned[0]:
        order += turned[0][:2] + lookups[:1]
        del turned[0][:2], lookups[:1]
    return order + lookups + turned[1]


EMB_ORDER = emb_order(False)
FIRST_ORDER = emb_order(True)
FIRST_PAIRS = 4
EMB_BATCHES = len(EMB_ORDER)
EMB_FIRST = EMB_BATCHES - -(-NG // TR_PER_BANK)


def before(n, banks, batches):
    return n - banks + 1 if n >= banks else max(range(n, batches, banks)) + 1 - batches


def order_of(p):
    return FIRST_ORDER if isinstance(p, int) and p < FIRST_PAIRS else EMB_ORDER


def is_early(order, n):
    return order[n][0] == 0


def banks_of_kind(order, n, early):
    return sum(is_early(order, m) == early for m in range(n))


def banks_until_looked_up(p, k):
    return 1 + order_of(p).index((None, k, 1))


def fold_copies():
    rounds = []
    for group in reversed(range(3)):
        copies = []
        for quad in range(NQ):
            columns = range(quad, COLUMNS, NQ)
            slots = [(group * GROUP + c) % NF for c in columns]
            starts = [n for n in range(len(slots)) if n == 0 or slots[n] < slots[n - 1]] + [len(slots)]
            for first, end in zip(starts, starts[1:]):
                copies.append((quad, first, end - first, (group + 1) * GROUP, slots[first]))
        rounds.append(copies)
    return rounds


def folded_pairs():
    seen, out = set(), []
    for c in range(COLUMNS):
        for row in range(NF):
            other = (row // GROUP * GROUP + c) % NF
            pair = frozenset((row, other))
            if row != other and pair not in seen:
                seen.add(pair)
                out.append((c, row, other))
    assert len(out) == NF * (NF - 1) // 2
    return out


def build(nc, dense_t, ids_rows, ids_onehot, gathered_tables, onehot_tables, w1, w2, w3, b1, b2, out):
    with ExitStack() as ctx:
        def sb(name, shape, dt=F32):
            return ctx.enter_context(nc.sbuf_tensor(name, shape, dt))

        def sem(name):
            return ctx.enter_context(nc.semaphore(name))

        idx = sb("idx", [P, 2, TILES * NG], I32)
        ids_b = sb("ids_b", [P, NO, PAIR], I32)
        rows = sb("rows", [P, TILES, NG, DIM])
        emb = sb("emb", [P, TILES, P, QUAD])
        gram = sb("gram", [P, GRAM_BATCHES, PER_BANK * GCOLS])
        folded = sb("folded", [P, 2, STEPS, PAIR])
        table_hi = sb("table_hi", [P, NO, ROWS_PER, DIM], F32R)
        table_lo = sb("table_lo", [P, NO, ROWS_PER, DIM], F32R)
        onehot = sb("onehot", [P, ONEHOT_RING, ROWS_PER, PAIR], F32R)
        row_id_i = sb("row_id_i", [P, ROWS_PER], I32)
        ident = sb("ident", [P, P])
        w1_sb = sb("w1_sb", [P, STEPS, HID1])
        w2_sb = sb("w2_sb", [P, M1, HID2])
        w3_sb = sb("w3_sb", [P, M2])
        b1_sb = sb("b1_sb", [P, M1])
        b2_sb = sb("b2_sb", [P, M2])
        h1 = sb("h1", [P, M1, PAIR])
        h2 = sb("h2", [P, M2, PAIR])
        y = sb("y", [1, 2, PAIR])
        spaces = [gram[:, :, :].rearrange("p a b -> p (a b)"), folded[:, :, :, :].rearrange("p a b c -> p (a b c)")]
        part = ROWS_PER * DIM
        stages = [space[0:ROWS, k:k + part] for space in spaces for k in range(0, space.shape[1] - part + 1, part)]

        gram_ps = [ctx.enter_context(nc.psum_tensor(f"gram_ps{i}", [P, 512], F32)) for i in range(GRAM_BANKS)]
        emb_ps = [ctx.enter_context(nc.psum_tensor(f"emb_ps{i}", [P, 512], F32)) for i in range(EMB_BANKS)]
        row_id = ctx.enter_context(nc.psum_tensor("row_id", [P, 512], F32))
        mlp_ps = [ctx.enter_context(nc.psum_tensor(f"mlp_ps{i}", [P, 512], F32)) for i in range(2)]

        idx_loaded = [sem(f"idx_loaded{i}") for i in range(2)]
        ids_b_loaded = sem("ids_b_loaded")
        dense_loaded = [sem(f"dense_loaded{i}") for i in range(2)]
        table_loaded = [sem(f"table_loaded{i}") for i in range(NO)]
        weights_loaded = sem("weights_loaded")
        gathered = [sem(f"gathered{i}") for i in range(TILES)]
        gather_begun = sem("gather_begun")
        ident_steps = sem("ident_steps")
        table_rounded = sem("table_rounded")
        table_split = sem("table_split")
        cleared = sem("cleared")
        onehot_ready = sem("onehot_ready")
        emb_ps_full = sem("emb_ps_full")
        early_taken = sem("early_taken")
        other_taken = sem("other_taken")
        gram_ps_full = sem("gram_ps_full")
        gram_ps_empty = sem("gram_ps_empty")
        folded_dve = sem("folded_dve")
        folded_act = sem("folded_act")
        mlp_full = sem("mlp_full")
        mlp_empty = sem("mlp_empty")
        y_stored = [sem(f"y_stored{i}") for i in range(2)]

        ROUNDS = fold_copies()
        NR = len(ROUNDS)
        LAST = PAIRS - 1
        LAST_MLP_CHUNKS = MLP_CHUNKS + M1
        BOTH = (0, TILES)

        def pair(i, c):
            return i * 2 + c, i + c // 2

        STARTED = 2

        def act_rounds_before(p, t=0):
            return (p * TILES + t) * NR if isinstance(p, int) and p < STARTED else (p + STARTED + t) * NR

        def dve_rounds_before(p, t=0):
            if isinstance(p, int) and p <= STARTED:
                return (p * TILES + t) * NR
            return (STARTED * TILES + 1 + t) * NR

        def dve_share(p, t):
            return NQ - 1 if t == 0 or p == LAST else NQ // 2

        def bank_taken(p, n, order):
            early = is_early(order, n)
            per_pair = banks_of_kind(order, EMB_BATCHES, early)
            return early_taken if early else other_taken, p * per_pair + banks_of_kind(order, n + 1, early)

        def bank_aps(p, n):
            t, first, size = order_of(p)[n]
            bank = emb_ps[n % EMB_BANKS]
            if t is None:
                return (emb[:, :, :, NG + first], bank[:, 0:PAIR].rearrange("d (t b) -> d t b", t=TILES))
            return (emb[:, t, :, first:first + size], bank[:, 0:size * P].rearrange("d (f b) -> d b f", f=size))

        def fold_aps(par, q, copy, t0, t1):
            quad, step, n, nrows, src = copy
            dst = folded[quad * QUAD:quad * QUAD + nrows, par, step:step + n, t0 * P:t1 * P].rearrange(
                "p n (b q) -> p n b q", q=NQ)[:, :, :, q]
            col = q * NF + src
            batches = GRAM_BATCHES // TILES
            products = gram[q * QUAD:q * QUAD + nrows, t0 * batches:t1 * batches, :].rearrange(
                "p a (b c) -> p c (a b)", c=GCOLS)
            return dst, products[:, col:col + NQ * (n - 1) + 1:NQ, :]

        block = ctx.enter_context(nc.Block())

        @block.sync
        def _(sp):
            def load_idx(p, par):
                sp.dma_start(idx[:, par, :], ids_rows[bass.ds(p, 1), :, :].rearrange("o p f -> (o p) f")
                             ).then_inc(idx_loaded[par], 16)

            def load_ids_b(p):
                sp.dma_start(ids_b[:], ids_onehot[:, bass.ds(p * PAIR, PAIR)].partition_broadcast(P)
                             ).then_inc(ids_b_loaded, 16)

            def load_dense(p, par):
                q, step = DENSE_COLUMN % NQ, DENSE_COLUMN // NQ
                sp.dma_start(folded[q * QUAD:q * QUAD + DENSE, par, step, :],
                             dense_t[:, bass.ds(p * PAIR, PAIR)]).then_inc(dense_loaded[par], 16)

            def next_ids_b(p):
                sp.wait_ge(onehot_ready, (p + 1) * NO)
                load_ids_b(p + 1)

            def next_idx(p, par):
                for t in range(TILES):
                    sp.wait_ge(gathered[t], (p + 1) * (16 * NG))
                load_idx(p + 2, par)

            def next_dense(p, par):
                sp.wait_ge(mlp_full, p * MLP_CHUNKS + M1)
                load_dense(p + 2, par)

            def store_y(p, par, chunks):
                sp.wait_ge(mlp_empty, p * MLP_CHUNKS + chunks)
                sp.dma_start(out[bass.ds(p * PAIR, PAIR), :].rearrange("n o -> o n"),
                             y[:, par, :]).then_inc(y_stored[par], 16)

            for par in range(2):
                sp.sem_inc(y_stored[par], 16)
            load_idx(0, 0)
            for n in range(NO):
                sp.dma_start(stages[n], onehot_tables[n].rearrange("(p j) d -> p (j d)", j=ROWS_PER)
                             ).then_inc(table_loaded[n], 16)
                if n == 0:
                    load_ids_b(0)
            load_idx(1, 1)
            for dst, src in ((w1_sb, w1), (w2_sb, w2), (w3_sb, w3), (b1_sb, b1), (b2_sb, b2)):
                sp.dma_start(dst[:], src).then_inc(weights_loaded, 16)
            sp.wait_ge(cleared, 3)
            load_dense(0, 0)
            load_dense(1, 1)
            next_ids_b(0)
            next_idx(0, 0)
            next_ids_b(1)
            next_idx(1, 1)
            next_dense(0, 0)
            with sp.Fori(1, PAIRS // 2 - 1) as i:
                for c in range(2):
                    p, _ = pair(i, c)
                    next_ids_b(p)
                    next_idx(p, c)
                    store_y(p - 2, c, MLP_CHUNKS)
                    next_dense(p - 1, (c - 1) % 2)
            next_ids_b(LAST - 1)
            store_y(LAST - 3, (LAST - 3) % 2, MLP_CHUNKS)
            next_dense(LAST - 2, (LAST - 2) % 2)
            store_y(LAST - 2, (LAST - 2) % 2, MLP_CHUNKS)
            store_y(LAST - 1, (LAST - 1) % 2, MLP_CHUNKS)
            store_y(LAST, LAST % 2, LAST_MLP_CHUNKS)
            for par in range(2):
                sp.wait_ge(y_stored[par], 16 * (PAIRS // 2 + 1))

        @block.gpsimd
        def _(pool):
            def gather(p, par, use):
                for t in range(TILES):
                    pool.wait_ge(idx_loaded[par], (use + 1) * 16)
                    if not (isinstance(p, int) and p == 0):
                        if t == 0:
                            pool.wait_ge(early_taken, p * (EMB_FIRST - NO))
                        else:
                            pool.wait_ge(emb_ps_full, p * EMB_BATCHES)
                    pool.sem_inc(gather_begun, 1)
                    for n in range(NG):
                        col = t * NG + n
                        pool.indirect_dma_start(
                            out=rows[:, t, n, :], out_offset=None, in_=gathered_tables[n],
                            in_offset=bass.IndirectOffsetOnAxis(ap=idx[:, par, col:col + 1], axis=0),
                        ).then_inc(gathered[t], 16)

            nc.gpsimd.memset(ident[:], 0.0).then_inc(ident_steps, 1)
            nc.gpsimd.iota(row_id_i[:], pattern=[[1, ROWS_PER]], base=0,
                           channel_multiplier=ROWS_PER).then_inc(ident_steps, 1)
            pool.wait_ge(ident_steps, 2)
            nc.gpsimd.affine_select(out=ident[:], in_=ident[:], compare_op=ALU.not_equal, fill=1.0,
                                    base=0, pattern=[[-1, P]], channel_multiplier=1).then_inc(ident_steps, 1)
            for p in range(FIRST_PAIRS):
                gather(p, p % 2, p // 2)
            with pool.Fori(FIRST_PAIRS // 2, PAIRS // 2) as i:
                for c in range(2):
                    p, use = pair(i, c)
                    gather(p, c, use)

        @block.tensor
        def _(pe):
            def embeddings(p, n0, n1):
                for n in range(n0, n1):
                    t, first, size = order_of(p)[n]
                    bank = emb_ps[n % EMB_BANKS]
                    if not (isinstance(p, int) and p == 0 and n < EMB_BANKS):
                        m = before(n, EMB_BANKS, EMB_BATCHES) - 1
                        if m < 0:
                            pe.wait_ge(*bank_taken(p - 1, m + EMB_BATCHES, order_of(p - 1)))
                        else:
                            pe.wait_ge(*bank_taken(p, m, order_of(p)))
                            if n0 == EMB_FIRST and not isinstance(p, int):
                                pe.wait_ge(*bank_taken(p, m, FIRST_ORDER))
                    if t is None:
                        pe.wait_ge(onehot_ready, p * NO + first + 1)
                        for j in range(ROWS_PER):
                            for part, table in enumerate((table_hi, table_lo)):
                                last = nc.tensor.matmul(bank[:, 0:PAIR], table[0:ROWS, first, j, :],
                                                        onehot[0:ROWS, first % ONEHOT_RING, j, :],
                                                        start=(j == 0 and part == 0),
                                                        stop=(j == ROWS_PER - 1 and part == 1))
                    else:
                        if first == 0:
                            pe.wait_ge(gathered[t], (p + 1) * (16 * NG))
                        for f in range(size):
                            last = nc.tensor.transpose(bank[:, f * P:(f + 1) * P],
                                                       rows[:, t, first + f, :], ident[:])
                    last.then_inc(emb_ps_full, 1)

            def gram_products(p, t0, t1, banks):
                for early, taken in ((True, early_taken), (False, other_taken)):
                    pe.wait_ge(taken, p * banks_of_kind(order_of(p), EMB_BATCHES, early)
                               + banks_of_kind(order_of(p), banks, early))
                for a in range(t0 * GRAM_BATCHES // TILES, t1 * GRAM_BATCHES // TILES):
                    if not (isinstance(p, int) and p == 0 and a < GRAM_BANKS):
                        pe.wait_ge(gram_ps_empty, p * GRAM_BATCHES + before(a, GRAM_BANKS, GRAM_BATCHES))
                    for b in range(PER_BANK):
                        t, g = divmod(a * PER_BANK + b, P // NQ)
                        samples = emb[:, t, g * NQ:(g + 1) * NQ, :]
                        last = nc.tensor.matmul(gram_ps[a % GRAM_BANKS][:, b * GCOLS:(b + 1) * GCOLS],
                                                samples.rearrange("d b s -> d (b s)"),
                                                samples[:, :, 0:NF], start=True, stop=True)
                    last.then_inc(gram_ps_full, 1)

            def layer1(par, t0, t1, chunks, odd, dve_rounds, act_rounds, loads):
                pe.wait_ge(folded_dve, dve_rounds)
                pe.wait_ge(folded_act, act_rounds)
                pe.wait_ge(dense_loaded[par], loads * 16)
                c0, c1 = t0 * P, t1 * P
                for m in range(M1):
                    if not (isinstance(chunks, int) and chunks + m < 2):
                        pe.wait_ge(mlp_empty, chunks + m - 1)
                    for s in range(STEPS):
                        last = nc.tensor.matmul(mlp_ps[(odd + m) % 2][:, c0:c1], w1_sb[:, s, m * P:(m + 1) * P],
                                                folded[:, par, s, c0:c1], start=(s == 0), stop=(s == STEPS - 1))
                    last.then_inc(mlp_full, 1)

            def layer2(chunks, odd, m0=0, m1=M2):
                if m0 == 0:
                    pe.wait_ge(mlp_empty, chunks)
                for m in range(m0, m1):
                    for k in range(M1):
                        last = nc.tensor.matmul(mlp_ps[(odd + m) % 2][:, 0:PAIR], w2_sb[:, k, m * P:(m + 1) * P],
                                                h1[:, k, :], start=(k == 0), stop=(k == M1 - 1))
                    last.then_inc(mlp_full, 1)

            def layer3(chunks, odd):
                pe.wait_ge(mlp_empty, chunks)
                for k in range(M2):
                    last = nc.tensor.matmul(mlp_ps[odd % 2][0:1, 0:PAIR], w3_sb[:, k:k + 1],
                                            h2[:, k, :], start=(k == 0), stop=(k == M2 - 1))
                last.then_inc(mlp_full, 1)

            def layer1_of_pair(p, use, par):
                layer1(par, *BOTH, p * MLP_CHUNKS, par * MLP_CHUNKS,
                       dve_rounds_before(p + 1), act_rounds_before(p + 1), use + 1)

            def layer2_of_pair(p, par, m0=0, m1=M2):
                layer2(p * MLP_CHUNKS + M1, par * MLP_CHUNKS + M1, m0, m1)

            def layer3_of_pair(p, par):
                layer3(p * MLP_CHUNKS + M1 + M2, par * MLP_CHUNKS + M1 + M2)

            pe.wait_ge(ident_steps, 3)
            pe.wait_ge(cleared, 1)
            embeddings(0, 0, EMB_FIRST)
            gram_products(0, 0, 1, EMB_FIRST)
            embeddings(0, EMB_FIRST, EMB_BATCHES)
            gram_products(0, 1, 2, EMB_BATCHES)
            embeddings(1, 0, EMB_FIRST)
            pe.wait_ge(weights_loaded, 5 * 16)
            layer1_of_pair(0, 0, 0)
            gram_products(1, 0, 1, EMB_FIRST)
            layer2_of_pair(0, 0, 0, M2 - 1)
            embeddings(1, EMB_FIRST, EMB_BATCHES)
            layer2_of_pair(0, 0, M2 - 1, M2)
            gram_products(1, 1, 2, EMB_BATCHES)
            embeddings(2, 0, EMB_FIRST)
            layer3_of_pair(0, 0)
            layer1_of_pair(1, 0, 1)
            embeddings(2, EMB_FIRST, EMB_BATCHES)
            gram_products(2, 0, 1, EMB_FIRST)
            gram_products(2, 1, 2, EMB_BATCHES)
            embeddings(3, 0, EMB_FIRST)
            with pe.Fori(1, PAIRS // 2 - 1) as i:
                for c in range(1, 3):
                    p, _ = pair(i, c)
                    layer2_of_pair(p - 2, c % 2, 0, M2 - 1)
                    gram_products(p, 0, 1, EMB_FIRST)
                    embeddings(p, EMB_FIRST, EMB_BATCHES)
                    layer2_of_pair(p - 2, c % 2, M2 - 1, M2)
                    gram_products(p, 1, 2, EMB_BATCHES)
                    layer3_of_pair(p - 2, c % 2)
                    layer1_of_pair(*pair(i, c - 1), (c - 1) % 2)
                    embeddings(p + 1, 0, EMB_FIRST)
            p = LAST - 1
            layer2_of_pair(p - 1, (p - 1) % 2)
            gram_products(LAST, 0, 1, EMB_FIRST)
            layer3_of_pair(p - 1, (p - 1) % 2)
            layer1_of_pair(p, p // 2, p % 2)
            embeddings(LAST, EMB_FIRST, EMB_BATCHES)
            layer2_of_pair(p, p % 2, 0, M2 - 1)
            gram_products(LAST, 1, 2, EMB_BATCHES)
            layer2_of_pair(p, p % 2, M2 - 1, M2)
            layer3_of_pair(p, p % 2)
            for t in range(TILES):
                chunks = LAST * MLP_CHUNKS + t * M1
                layer1(LAST % 2, t, t + 1, chunks, chunks,
                       dve_rounds_before(LAST, t + 1), act_rounds_before(LAST, t + 1), PAIRS // 2)
            chunks = LAST * MLP_CHUNKS + TILES * M1
            layer2(chunks, chunks)
            layer3(chunks + M2, chunks + M2)

        @block.vector
        def _(dve):
            def make_onehots(p, tables):
                dve.wait_ge(ids_b_loaded, (p + 1) * 16)
                for k in tables:
                    slot = k % ONEHOT_RING
                    if k >= ONEHOT_RING:
                        dve.wait_ge(emb_ps_full, p * EMB_BATCHES + banks_until_looked_up(p, k - ONEHOT_RING))
                    elif not (isinstance(p, int) and p == 0):
                        user = max(range(slot, NO, ONEHOT_RING))
                        dve.wait_ge(emb_ps_full, (p - 1) * EMB_BATCHES + banks_until_looked_up(p - 1, user))
                    nc.vector.tensor_tensor(
                        onehot[0:ROWS, slot, :, :],
                        ids_b[0:ROWS, k, :].unsqueeze(1).broadcast_to([ROWS, ROWS_PER, PAIR]),
                        row_id[0:ROWS, 0:ROWS_PER].unsqueeze(2).broadcast_to([ROWS, ROWS_PER, PAIR]),
                        ALU.is_equal).then_inc(onehot_ready, 1)

            def fold(par, t0, t1, batches, rounds, samples):
                dve.wait_ge(gram_ps_empty, batches)
                for r, copies in enumerate(ROUNDS):
                    if r:
                        dve.wait_ge(folded_dve, rounds + r)
                    for q in range(samples):
                        for copy in copies:
                            dst, src = fold_aps(par, q, copy, t0, t1)
                            last = nc.vector.tensor_copy(dst, src)
                    last.then_inc(folded_dve, 1)

            def fold_tile(p, par, t):
                fold(par, t, t + 1, p * GRAM_BATCHES + (t + 1) * GRAM_BATCHES // TILES,
                     dve_rounds_before(p, t), dve_share(p, t))

            def take_embeddings(p, n0, n1):
                for n in range(n0, n1):
                    t, k, _ = order_of(p)[n]
                    if not is_early(order_of(p), n):
                        dve.wait_ge(emb_ps_full, p * EMB_BATCHES + n + 1)
                        nc.vector.tensor_copy(*bank_aps(p, n)).then_inc(other_taken, 1)
                        if t is None and k + ONEHOT_RING < NO:
                            make_onehots(p, [k + ONEHOT_RING])

            nc.vector.memset(emb[:, :, :, NF:QUAD], 0.0).then_inc(cleared, 1)
            dve.wait_ge(ident_steps, 2)
            nc.vector.tensor_copy(row_id[:, 0:ROWS_PER], row_id_i[:]).then_inc(cleared, 1)
            dve.wait_ge(cleared, 2)
            for n in range(NO):
                dve.wait_ge(table_loaded[n], 16)
                dve.wait_ge(table_rounded, n + 1)
                nc.vector.tensor_tensor(table_lo[0:ROWS, n, :, :].rearrange("p j d -> p (j d)"), stages[n],
                                        table_hi[0:ROWS, n, :, :].rearrange("p j d -> p (j d)").bitcast(F32),
                                        ALU.subtract).then_inc(table_split, 1)
                make_onehots(0, [n])
            dve.wait_ge(table_split, NO)
            nc.vector.memset(folded[:], 0.0).then_inc(cleared, 1)
            dve.wait_ge(cleared, 3)
            make_onehots(1, range(ONEHOT_RING))
            for t in range(TILES):
                fold_tile(0, 0, t)
            make_onehots(1, range(ONEHOT_RING, NO))
            make_onehots(2, range(ONEHOT_RING))
            for t in range(TILES):
                fold_tile(1, 1, t)
            make_onehots(2, range(ONEHOT_RING, NO))
            make_onehots(3, range(ONEHOT_RING))
            take_embeddings(3, 0, EMB_FIRST)
            fold(0, *BOTH, 3 * GRAM_BATCHES, dve_rounds_before(2), 1)
            with dve.Fori(1, PAIRS // 2 - 1) as i:
                for c in range(1, 3):
                    p, _ = pair(i, c)
                    take_embeddings(p, EMB_FIRST, EMB_BATCHES)
                    make_onehots(p + 1, range(ONEHOT_RING))
                    take_embeddings(p + 1, 0, EMB_FIRST)
            fold_tile(LAST, LAST % 2, 0)
            take_embeddings(LAST, EMB_FIRST, EMB_BATCHES)
            fold_tile(LAST, LAST % 2, 1)

        @block.scalar
        def _(act):
            def take_bank(p, n):
                act.wait_ge(emb_ps_full, p * EMB_BATCHES + n + 1)
                nc.scalar.copy(*bank_aps(p, n)).then_inc(early_taken if is_early(order_of(p), n) else other_taken, 1)

            def take_embeddings(p, n0, n1):
                for n in range(n0, n1):
                    take_bank(p, n)

            def take_gram(p, t0, t1):
                for a in range(t0 * GRAM_BATCHES // TILES, t1 * GRAM_BATCHES // TILES):
                    if a == 0 and p > 0:
                        act.wait_ge(folded_dve, dve_rounds_before(p))
                        act.wait_ge(folded_act, act_rounds_before(p))
                    act.wait_ge(gram_ps_full, p * GRAM_BATCHES + a + 1)
                    nc.scalar.copy(gram[:, a, :], gram_ps[a % GRAM_BANKS][:, 0:PER_BANK * GCOLS]
                                   ).then_inc(gram_ps_empty, 1)

            def take_layer(layer, m, par, t0, t1, chunks, odd, stores=0):
                c0, c1 = t0 * P, t1 * P
                src = mlp_ps[odd % 2]
                act.wait_ge(mlp_full, chunks + 1)
                if layer == 1:
                    nc.scalar.activation(h1[:, m, c0:c1], src[:, c0:c1], ACT.Relu,
                                         bias=b1_sb[:, m:m + 1]).then_inc(mlp_empty, 1)
                elif layer == 2:
                    nc.scalar.activation(h2[:, m, c0:c1], src[:, c0:c1], ACT.Relu,
                                         bias=b2_sb[:, m:m + 1]).then_inc(mlp_empty, 1)
                else:
                    act.wait_ge(y_stored[par], (stores + 1) * 16)
                    nc.scalar.copy(y[:, par, c0:c1], src[0:1, c0:c1]).then_inc(mlp_empty, 1)

            def take_layer1(p, par, m):
                take_layer(1, m, par, *BOTH, p * MLP_CHUNKS + m, par * MLP_CHUNKS + m)

            def take_layer2_chunk(p, par, m):
                take_layer(2, m, par, *BOTH, p * MLP_CHUNKS + M1 + m, par * MLP_CHUNKS + M1 + m)

            def take_layer2(p, par):
                for m in range(M2):
                    take_layer2_chunk(p, par, m)

            def take_layer3(p, use, par):
                chunk = M1 + M2
                take_layer(3, 0, par, *BOTH, p * MLP_CHUNKS + chunk, par * MLP_CHUNKS + chunk, use)

            def fold(par, t0, t1, batches, rounds, samples, takes, take):
                taken = done = 0
                act.wait_ge(gram_ps_empty, batches)
                for r, copies in enumerate(ROUNDS):
                    if r:
                        act.wait_ge(folded_act, rounds + r)
                    for q in samples:
                        for copy in copies:
                            dst, src = fold_aps(par, q, copy, t0, t1)
                            last = nc.scalar.copy(dst, src)
                            done += 1
                            if copy is copies[-1] and q == samples[-1]:
                                last.then_inc(folded_act, 1)
                            if taken < len(takes) and done >= takes[taken]:
                                take(taken)
                                taken += 1
                assert taken == len(takes)

            def fold_tile(p, par, t, takes, take):
                fold(par, t, t + 1, p * GRAM_BATCHES + (t + 1) * GRAM_BATCHES // TILES,
                     act_rounds_before(p, t), range(dve_share(p, t), NQ), takes, take)

            def fold_pair(p, par, before, before_par):
                banks = [n for n, (t, _, _) in enumerate(EMB_ORDER) if t == 0]
                assert len(TAKES_OF_FOLD) == M1 + len(banks)

                def take(n):
                    if n < M1:
                        take_layer1(before, before_par, n)
                    else:
                        take_bank(p + 1, banks[n - M1])

                fold(par, *BOTH, (p + 1) * GRAM_BATCHES, act_rounds_before(p), range(NQ), TAKES_OF_FOLD, take)

            for n in range(NO):
                act.wait_ge(table_loaded[n], 16)
                nc.scalar.copy(table_hi[0:ROWS, n, :, :].rearrange("p j d -> p (j d)"), stages[n]
                               ).then_inc(table_rounded, 1)
            act.wait_ge(cleared, 1)
            take_embeddings(0, 0, EMB_FIRST)
            act.wait_ge(table_split, NO)
            act.wait_ge(cleared, 3)
            take_gram(0, 0, 1)
            fold_tile(0, 0, 0, range(12, 12 + EMB_BATCHES - EMB_FIRST), lambda n: take_bank(0, EMB_FIRST + n))
            take_gram(0, 1, 2)
            fold_tile(0, 0, 1, range(6, 6 * ONEHOT_RING + 1, 6), lambda n: take_bank(1, n))
            take_embeddings(1, ONEHOT_RING, EMB_FIRST)
            act.wait_ge(weights_loaded, 5 * 16)
            for m in range(M1):
                take_layer1(0, 0, m)
            take_gram(1, 0, 1)
            last_banks = EMB_BATCHES - EMB_FIRST

            def take_between(n):
                if n in (0, 1 + last_banks):
                    take_layer2_chunk(0, 0, 0 if n == 0 else 1)
                else:
                    take_bank(1, EMB_FIRST + n - 1)

            fold_tile(1, 1, 0, range(4, 4 + M2 + last_banks), take_between)
            take_gram(1, 1, 2)
            fold_tile(1, 1, 1, range(6, 6 * ONEHOT_RING + 1, 6), lambda n: take_bank(2, n))
            take_embeddings(2, ONEHOT_RING, EMB_FIRST)
            take_layer3(0, 0, 0)
            for m in range(M1):
                take_layer1(1, 1, m)
            take_embeddings(2, EMB_FIRST, EMB_BATCHES)
            take_gram(2, *BOTH)
            fold(0, *BOTH, 3 * GRAM_BATCHES, act_rounds_before(2), range(1, NQ),
                 range(43, 43 + EMB_FIRST - NO), lambda n: take_bank(3, NO + n))
            with act.Fori(1, PAIRS // 2 - 1) as i:
                for c in range(1, 3):
                    p, _ = pair(i, c)
                    take_layer2_chunk(p - 2, c % 2, 0)
                    take_gram(p, 0, 1)
                    take_layer2_chunk(p - 2, c % 2, 1)
                    take_gram(p, 1, 2)
                    take_layer3(*pair(i, c - 2), c % 2)
                    fold_pair(p, c % 2, p - 1, (c - 1) % 2)
            p = LAST - 1
            take_layer2(p - 1, (p - 1) % 2)
            par = LAST % 2

            def late_layers(n):
                if n == 0:
                    take_layer2_chunk(p, p % 2, M2 - 1)
                else:
                    take_layer3(p, p // 2, p % 2)

            take_gram(LAST, 0, 1)
            take_layer3(p - 1, (p - 1) // 2, (p - 1) % 2)
            fold_tile(LAST, par, 0, range(3, 3 * M1 + 1, 3), lambda m: take_layer1(p, p % 2, m))
            take_layer2_chunk(p, p % 2, 0)
            take_gram(LAST, 1, 2)
            fold_tile(LAST, par, 1, (6, 12), late_layers)
            chunks = LAST * MLP_CHUNKS
            for t in range(TILES):
                for m in range(M1):
                    take_layer(1, m, par, t, t + 1, chunks, chunks)
                    chunks += 1
            for m in range(M2):
                take_layer(2, m, par, *BOTH, chunks, chunks)
                chunks += 1
            take_layer(3, 0, par, *BOTH, chunks, chunks, LAST // 2)



def layer1_layout(w):
    laid = np.zeros((STEPS, P, HID1), w.dtype)
    for c, row, other in folded_pairs():
        i, j = sorted((SLOT_FEATURE[row], SLOT_FEATURE[other]))
        n = i * NF - i * (i + 1) // 2 + (j - i - 1)
        laid[c // NQ, (c % NQ) * QUAD + row] = w[n]
    q = DENSE_COLUMN % NQ
    laid[DENSE_COLUMN // NQ, q * QUAD:q * QUAD + DENSE] = w[NF * (NF - 1) // 2:]
    return laid.transpose(1, 0, 2)


def kernel(**inputs):
    import concourse.bacc as bacc
    from concourse.bass_utils import run_bass_kernel_spmd

    a = {k: np.asarray(v) for k, v in inputs.items()}
    ids = a["ids"]
    nc = bacc.Bacc("TRN2", target_bir_lowering=False, num_devices=1)
    arrays = {}

    def dram(name, array):
        arrays[name] = np.ascontiguousarray(array)
        return nc.dram_tensor(name, arrays[name].shape, mybir.dt.from_np(arrays[name].dtype),
                              kind="ExternalInput").ap()

    out = nc.dram_tensor("out", (BATCH, 1), F32, kind="ExternalOutput").ap()
    build(
        nc,
        dram("dense_t", a["dense_ctx"].T),
        dram("ids_rows", ids[:, GATHERED].reshape(PAIRS, TILES, P, NG).transpose(0, 2, 1, 3)
             .reshape(PAIRS, P, TILES * NG)),
        dram("ids_onehot", ids[:, ONEHOT].T),
        [dram(f"tbl_{f}_rows", a[f"tbl_{f}"]) for f in GATHERED],
        [dram(f"tbl_{f}_rows", a[f"tbl_{f}"]) for f in ONEHOT],
        dram("w1", layer1_layout(a["W_top1"])),
        dram("w2", a["W_top2"].reshape(M1, P, HID2).transpose(1, 0, 2)),
        dram("w3", a["W_top3"].reshape(M2, P).T),
        dram("b1", a["b_top1"].reshape(M1, P).T),
        dram("b2", a["b_top2"].reshape(M2, P).T),
        out,
    )
    r = run_bass_kernel_spmd(nc, [arrays], core_ids=[0])
    return r.results[0]["out"]
```
